# Optimizing a Trainium2 kernel written in Bass

```python
import numpy as np
import jax
import jax.numpy as jnp

def _softmax(x, axis=-1):
    return jax.nn.softmax(x, axis=axis)

def _gelu(x):
    return jax.nn.gelu(x, approximate=True)

def _silu(x):
    return jax.nn.silu(x)

def _sigmoid(x):
    return jax.nn.sigmoid(x)

def _layernorm(x, axis=-1, eps=1e-05):
    m = jnp.mean(x, axis=axis, keepdims=True)
    v = jnp.var(x, axis=axis, keepdims=True)
    return (x - m) / jnp.sqrt(v + eps)

def _scatter_add(tgt, idx, src, axis=0):
    return tgt.at[idx].add(src)

def _segment_sum(src, seg, n):
    return jax.ops.segment_sum(src, seg, n)
kernel_name = 'mk_prb_d1_jaxref_r8_38553f'

def setup_inputs(seed: int=0):
    np.random.seed(seed)
    _w = jnp.asarray

    def _L0_attn_setup():
        import jax, jax.numpy as jnp
        import numpy as np
        N_EMBD = 128
        N_HEAD = 16
        HORIZON = 64
        HS = N_EMBD // N_HEAD
        BD = max(HS // 4, 16)

        def _windows(t, delta):
            B, nh, T, D = t.shape
            padded = jnp.pad(t, ((0, 0), (0, 0), (delta - 1, 0), (0, 0)))
            idx = jnp.arange(T)[:, None] + jnp.arange(delta)[None, :]
            return padded[:, :, idx]
        key = jax.random.key(seed)
        ks = jax.random.split(key, 12)
        s = 0.02
        B, T = (2, 128)
        return {'x': jax.random.normal(ks[0], (B, T, N_EMBD), jnp.float32), 'W_disp': jax.random.normal(ks[1], (N_EMBD, N_HEAD * BD), jnp.float32) * s, 'W_val': jax.random.normal(ks[2], (N_EMBD, N_EMBD), jnp.float32) * s, 'rel_pos_emb': jax.random.normal(ks[3], (HORIZON, BD), jnp.float32) * s, 'W_strain': jax.random.normal(ks[4], (BD, BD), jnp.float32) * s, 'W_pos': jax.random.normal(ks[5], (BD, BD), jnp.float32) * s, 'W_bond': jax.random.normal(ks[6], (BD, 1), jnp.float32) * s, 'W_dmg': jax.random.normal(ks[7], (BD, BD), jnp.float32) * s, 'b_dmg': jnp.zeros((BD,), jnp.float32), 'W_dmg_out': jax.random.normal(ks[8], (BD, 1), jnp.float32) * s, 'b_dmg_out': jnp.full((1,), -3.0, jnp.float32), 'W_cproj': jax.random.normal(ks[9], (N_EMBD, N_EMBD), jnp.float32) * s}
    _L0_attn_in = _L0_attn_setup()

    def _L0_ffn_setup():
        import jax, jax.numpy as jnp
        import numpy as np
        NUM_EXPERTS = 160
        TOP_K = 8
        ROUTED_SCALE = 2.5
        HIDDEN = 128
        INTER = 64
        key = jax.random.key(seed)
        ks = jax.random.split(key, 7)
        B, S = (1, 256)
        return {'hidden_states': jax.random.normal(ks[0], (B, S, HIDDEN), dtype=jnp.float32), 'router_w': jax.random.normal(ks[1], (NUM_EXPERTS, HIDDEN), dtype=jnp.float32) * 0.02, 'expert_bias': jnp.zeros((NUM_EXPERTS,), dtype=jnp.float32), 'w_gate': jax.random.normal(ks[2], (NUM_EXPERTS, INTER, HIDDEN), dtype=jnp.float32) * 0.02, 'w_down': jax.random.normal(ks[3], (NUM_EXPERTS, HIDDEN, INTER), dtype=jnp.float32) * 0.02, 'w_gate_shared': jax.random.normal(ks[4], (INTER, HIDDEN), dtype=jnp.float32) * 0.02, 'w_down_shared': jax.random.normal(ks[5], (HIDDEN, INTER), dtype=jnp.float32) * 0.02}
    _L0_ffn_in = _L0_ffn_setup()
    _d = {'L0_attn_x': _L0_attn_in['x'], 'L0_attn_W_disp': _L0_attn_in['W_disp'], 'L0_attn_W_val': _L0_attn_in['W_val'], 'L0_attn_rel_pos_emb': _L0_attn_in['rel_pos_emb'], 'L0_attn_W_strain': _L0_attn_in['W_strain'], 'L0_attn_W_pos': _L0_attn_in['W_pos'], 'L0_attn_W_bond': _L0_attn_in['W_bond'], 'L0_attn_W_dmg': _L0_attn_in['W_dmg'], 'L0_attn_b_dmg': _L0_attn_in['b_dmg'], 'L0_attn_W_dmg_out': _L0_attn_in['W_dmg_out'], 'L0_attn_b_dmg_out': _L0_attn_in['b_dmg_out'], 'L0_attn_W_cproj': _L0_attn_in['W_cproj'], 'L0_ffn_router_w': _L0_ffn_in['router_w'], 'L0_ffn_expert_bias': _L0_ffn_in['expert_bias'], 'L0_ffn_w_gate': _L0_ffn_in['w_gate'], 'L0_ffn_w_down': _L0_ffn_in['w_down'], 'L0_ffn_w_gate_shared': _L0_ffn_in['w_gate_shared'], 'L0_ffn_w_down_shared': _L0_ffn_in['w_down_shared']}
    _x0 = _d['L0_attn_x']
    _d['L0_attn_x'] = jax.random.normal(jax.random.fold_in(jax.random.key(seed), 1), (8, 1024, 128), dtype=_x0.dtype)
    del _x0
    return _d

def reference(L0_attn_x, L0_attn_W_disp, L0_attn_W_val, L0_attn_rel_pos_emb, L0_attn_W_strain, L0_attn_W_pos, L0_attn_W_bond, L0_attn_W_dmg, L0_attn_b_dmg, L0_attn_W_dmg_out, L0_attn_b_dmg_out, L0_attn_W_cproj, L0_ffn_router_w, L0_ffn_expert_bias, L0_ffn_w_gate, L0_ffn_w_down, L0_ffn_w_gate_shared, L0_ffn_w_down_shared):

    def _L0_attn_ref(x, W_disp, W_val, rel_pos_emb, W_strain, W_pos, W_bond, W_dmg, b_dmg, W_dmg_out, b_dmg_out, W_cproj):
        import jax, jax.numpy as jnp
        import numpy as np
        N_EMBD = 128
        N_HEAD = 16
        HORIZON = 64
        HS = N_EMBD // N_HEAD
        BD = max(HS // 4, 16)

        def _windows(t, delta):
            B, nh, T, D = t.shape
            padded = jnp.pad(t, ((0, 0), (0, 0), (delta - 1, 0), (0, 0)))
            idx = jnp.arange(T)[:, None] + jnp.arange(delta)[None, :]
            return padded[:, :, idx]
        B, T, C = x.shape
        nh, bd, hs = (N_HEAD, BD, HS)
        delta = min(HORIZON, T)
        disp = (x @ W_disp).reshape(B, T, nh, bd).transpose(0, 2, 1, 3)
        val = (x @ W_val).reshape(B, T, nh, hs).transpose(0, 2, 1, 3)
        disp_win = _windows(disp, delta)
        val_win = _windows(val, delta)
        cmask = jnp.arange(T)[:, None] - delta + 1 + jnp.arange(delta)[None, :] >= 0
        strain = disp_win - disp[:, :, :, None, :]
        rel_emb = rel_pos_emb[:delta]
        bond_act = jax.nn.gelu(strain @ W_strain + rel_emb @ W_pos, approximate=False)
        bond_logits = (bond_act @ W_bond)[..., 0]
        damage_act = jax.nn.gelu(strain @ W_dmg + b_dmg, approximate=False)
        damage = jax.nn.sigmoid((damage_act @ W_dmg_out)[..., 0] + b_dmg_out[0])
        logits = bond_logits - 10.0 * damage
        logits = jnp.where(cmask[None, None], logits, -jnp.inf)
        weights = jax.nn.softmax(logits, axis=-1)
        out = jnp.einsum('bntd,bntde->bnte', weights, val_win)
        out = out.transpose(0, 2, 1, 3).reshape(B, T, C)
        return out @ W_cproj

    def _L0_ffn_ref(hidden_states, router_w, expert_bias, w_gate, w_down, w_gate_shared, w_down_shared):
        import jax, jax.numpy as jnp
        import numpy as np
        NUM_EXPERTS = 160
        TOP_K = 8
        ROUTED_SCALE = 2.5
        HIDDEN = 128
        INTER = 64
        B, S, H = hidden_states.shape
        x = hidden_states.reshape(-1, H)
        T = x.shape[0]
        logits = x @ router_w.T + expert_bias[None, :]
        probs = jax.nn.sigmoid(logits)
        top_w, top_idx = jax.lax.top_k(probs, TOP_K)
        top_w = top_w / (jnp.sum(top_w, axis=-1, keepdims=True) + 1e-09)
        top_w = top_w * ROUTED_SCALE
        combine = jnp.zeros((T, NUM_EXPERTS), dtype=x.dtype)
        combine = combine.at[jnp.arange(T)[:, None], top_idx].set(top_w)
        h1 = jax.nn.silu(jnp.einsum('th,eih->eti', x, w_gate))
        h1w = h1 * combine.T[:, :, None]
        routed = jnp.einsum('eti,ehi->th', h1w, w_down)
        shared = jax.nn.silu(x @ w_gate_shared.T) @ w_down_shared.T
        return (routed + shared).reshape(B, S, H)
    x = L0_attn_x
    xn = _layernorm(x, axis=-1)
    x = x + _L0_attn_ref(xn, L0_attn_W_disp, L0_attn_W_val, L0_attn_rel_pos_emb, L0_attn_W_strain, L0_attn_W_pos, L0_attn_W_bond, L0_attn_W_dmg, L0_attn_b_dmg, L0_attn_W_dmg_out, L0_attn_b_dmg_out, L0_attn_W_cproj) + _L0_ffn_ref(xn, L0_ffn_router_w, L0_ffn_expert_bias, L0_ffn_w_gate, L0_ffn_w_down, L0_ffn_w_gate_shared, L0_ffn_w_down_shared)
    return x

_drawn_inputs = setup_inputs


def setup_inputs(seed=0):
    import zlib

    import numpy as np

    out = dict(_drawn_inputs(seed))
    spreads = {'L0_attn_b_dmg': (0.0, 2.0), 'L0_ffn_expert_bias': (0.0, 0.57)}
    factors = {'L0_attn_W_disp': 8.0,
     'L0_attn_W_val': 7.937,
     'L0_attn_rel_pos_emb': 8.0,
     'L0_attn_W_strain': 8.0,
     'L0_attn_W_pos': 8.0,
     'L0_attn_W_bond': 8.0,
     'L0_attn_W_dmg': 8.0,
     'L0_attn_W_dmg_out': 8.0,
     'L0_attn_W_cproj': 7.934,
     'L0_ffn_router_w': 3.647,
     'L0_ffn_w_gate': 3.484,
     'L0_ffn_w_down': 3.466,
     'L0_ffn_w_gate_shared': 3.078,
     'L0_ffn_w_down_shared': 3.043}
    for name, (base, spread) in spreads.items():
        noise = np.random.default_rng([zlib.crc32(name.encode()), seed]).standard_normal(out[name].shape)
        drawn = base * np.exp(spread * noise) if base else spread * noise
        out[name] = jnp.asarray(drawn.astype(out[name].dtype))
    for name, factor in factors.items():
        out[name] = (out[name] * factor).astype(out[name].dtype)
    return out
```

```python
from contextlib import ExitStack

import concourse.bass as bass
from concourse import mybir

F32 = mybir.dt.float32
BF16 = mybir.dt.bfloat16
I32 = mybir.dt.int32
U32 = mybir.dt.uint32
ALU = mybir.AluOpType
ACT = mybir.ActivationFunctionType
AX = mybir.AxisListType

P = 128
NEG = -1.0e30
LN_EPS = 1e-5
GATE_EPS = 1e-9
ROUTED_SCALE = 2.5
TOPK = 8


def moe_attention_layer(nc, x, w_dispT, w_val, relT, w_strain, w_pos, w_bond, w_dmg, b_dmg,
                        w_dmg_out, b_dmg_out, w_cproj, router_wT, expert_bias, w_expert,
                        w_gate_sharedT, w_down_sharedT, out):
    B, T, C = x.shape
    D, E = relT.shape[1], relT.shape[0]
    H = w_dispT.shape[0] // E
    HS = C // H
    NE = router_wT.shape[1]
    I = w_gate_sharedT.shape[1]
    HG = 2
    HH = H // HG
    TC = 512
    CB = T // TC
    NCH = B * CB
    J = TC // P
    NBLK = NCH * J
    NTOK = B * T
    PAD = D
    SW = TC + PAD
    NTILE = NTOK * TOPK // P + NE
    NSLOT = NTILE * P
    TB = 3
    NEST = NTILE // TB
    BANDW = P * HH
    HALF = P // 2
    assert C == P and HH * E == P and D == HALF and NTILE % (2 * TB) == 0

    with ExitStack() as ctx:
        def dram(name, shape, dt=F32):
            return nc.dram_tensor(name, shape, dt).ap()

        def sem(name):
            return ctx.enter_context(nc.semaphore(name))

        s_dram = dram("s_dram", (2 * HG, B, P, PAD + T))
        val_dram = dram("val_dram", (B, PAD + T + PAD, C))
        xn_dram = dram("xn_dram", (NTOK, C))
        rank_dram = dram("rank_dram", (NTOK, NE))
        part_dram = dram("part_dram", (NTOK, C))
        attn_dram = dram("attn_dram", (NTOK, C))
        band_dram = dram("band_dram", (2, J, P, BANDW))
        mask_dram = dram("mask_dram", (CB, P, D))
        tile_expert_dram = dram("tile_expert_dram", (1, 6 * P), I32)
        xslot_dram = dram("xslot_dram", (NSLOT, C))
        yslot_dram = dram("yslot_dram", (NSLOT, C))
        x_rows = x.rearrange("b t c -> (b t) c")
        out_rows = out.rearrange("b t c -> (b t) c")

        def chunk_rows(t, it):
            return t[bass.ds(it * TC, TC), :].rearrange("(j p) c -> p j c", p=P)

        held = sem("held")

        def after(e, s, n):
            if not isinstance(n, int) or n > 0:
                e.wait_ge(s, n)

        def hold(e, s, n):
            if not isinstance(n, int) or n > 0:
                e.wait_ge(s, n)
                e.sem_inc(held, 1)

        def peeled(e, n, body):
            body(0)
            with e.Fori(1, n) as i:
                body(i)

        def sb(name, shape, dt=F32, c=ctx):
            return c.enter_context(nc.sbuf_tensor(name, shape, dt))

        ident = sb("ident", [P, P])
        gates_all = sb("gates_all", [P, NBLK * TOPK])
        expert_all = sb("expert_all", [P, NBLK * TOPK])
        slots_all = sb("slots_all", [P, NBLK * TOPK], U32)
        w1 = sb("w1", [P, 2 * HG, P])
        wval_sb = sb("wval_sb", [P, C])
        wr_sb = sb("wr_sb", [P, NE])
        bias_sb = sb("bias_sb", [P, NE])
        wgs_sb = sb("wgs_sb", [P, I])
        wds_sb = sb("wds_sb", [I, C])
        wc_sb = sb("wc_sb", [P, C])
        rpos = sb("rpos", [P, D])
        bdmg_sb = sb("bdmg_sb", [P, 1])
        hbout = sb("hbout", [P, 1])
        wsel = sb("wsel", [P, 2, 4, 32])
        tri = sb("tri", [P, P], BF16)
        ones = sb("ones", [P, P], BF16)
        carry = sb("carry", [P, NE])
        iota_e = sb("iota_e", [P, NE])
        tile_id = sb("tile_id", [P, 6])
        mhalf = sb("mhalf", [P, J])

        with ExitStack() as c:
            zero = sb("zero", [P, 2048], F32, c)
            mask_sb = sb("mask_sb", [P, D], F32, c)
            bm = sb("bm", [P, HH], F32, c)
            wdT = sb("wdT", [P, HG, C], F32, c)
            bd = sb("bd", [P, 2, P], F32, c)
            wst = sb("wst", [P, 2, E], F32, c)
            wcol = sb("wcol", [P, 2], F32, c)
            wpos_sb = sb("wpos_sb", [E, P], F32, c)
            rel_sb = sb("rel_sb", [E, D], F32, c)
            bout_sb = sb("bout_sb", [P, 1], F32, c)
            psw = c.enter_context(nc.psum_tensor("psw", [P, 5, 512], F32))
            loaded = sem("const_loaded")
            zeroed = sem("const_zeroed")
            filled = sem("const_filled")
            pool_step = sem("const_pool_step")
            blockmask_ready = sem("blockmask_ready")
            bd_ready = sem("bd_ready")
            w1_done = sem("w1_done")
            with nc.Block() as block:
                @block.sync
                def _(sp):
                    for dst, src in ((wdT[:], w_dispT.rearrange("(g p) c -> p g c", p=P)), (wval_sb[:], w_val),
                                     (wst[:, 0, :], w_strain), (wst[:, 1, :], w_dmg), (wcol[:, 0:1], w_bond),
                                     (wcol[:, 1:2], w_dmg_out), (wpos_sb[:], w_pos), (rel_sb[:], relT),
                                     (bout_sb[:], b_dmg_out), (bdmg_sb[:], b_dmg), (wr_sb[:], router_wT),
                                     (wgs_sb[:], w_gate_sharedT), (wds_sb[:], w_down_sharedT),
                                     (wc_sb[:], w_cproj), (bias_sb[:], expert_bias.partition_broadcast(P))):
                        sp.dma_start(dst, src).then_inc(loaded, 16)
                    sp.wait_ge(zeroed, 1)
                    nfill = NSLOT * C // P // 2048
                    sp.dma_start(xslot_dram.rearrange("(p r) c -> p (r c)", p=P).rearrange("p (n f) -> p n f", n=nfill),
                                 zero[:].unsqueeze(1).to_broadcast([P, nfill, 2048])).then_inc(filled, 16)
                    sp.dma_start(band_dram.rearrange("s j p f -> p (s j) f"),
                                 zero[:, 0:BANDW].unsqueeze(1).to_broadcast([P, 2 * J, BANDW])).then_inc(filled, 16)
                    for i in range(2 * HG):
                        sp.dma_start(s_dram[i, :, :, 0:PAD].rearrange("b p t -> p b t"),
                                     zero[:, 0:B * PAD].rearrange("p (b t) -> p b t", b=B)).then_inc(filled, 16)
                    for lo in (0, PAD + T):
                        sp.dma_start(val_dram[:, lo:lo + PAD, :].rearrange("b p c -> p b c"),
                                     zero[0:PAD, 0:B * C].rearrange("p (b c) -> p b c", b=B)).then_inc(filled, 16)
                    sp.dma_start(mask_dram[1:CB].rearrange("n p d -> p n d"),
                                 zero[:, 0:(CB - 1) * D].rearrange("p (n d) -> p n d", n=CB - 1)).then_inc(filled, 16)
                    sp.wait_ge(pool_step, 6)
                    sp.dma_start(mask_dram[0], mask_sb[:]).then_inc(filled, 16)
                    sp.wait_ge(filled, 16 * (2 + 2 * HG + 2 + 2))

                @block.gpsimd
                def _(pool):
                    pool.memset(bm[:], 1.0).then_inc(pool_step, 1)
                    pool.wait_ge(pool_step, 1)
                    pool.affine_select(out=bm[:], in_=bm[:], compare_op=ALU.is_ge, fill=0.0, base=0,
                                       pattern=[[-E, HH]], channel_multiplier=1).then_inc(pool_step, 1)
                    pool.wait_ge(pool_step, 2)
                    pool.affine_select(out=bm[:], in_=bm[:], compare_op=ALU.is_ge, fill=0.0, base=E - 1,
                                       pattern=[[E, HH]], channel_multiplier=-1).then_inc(blockmask_ready, 1)
                    pool.memset(ident[:], 0.0).then_inc(pool_step, 1)
                    pool.memset(mask_sb[:], 0.0).then_inc(pool_step, 1)
                    pool.memset(tri[:], 1.0)
                    pool.memset(ones[:], 1.0)
                    pool.memset(mhalf[:], -0.5).then_inc(pool_step, 1)
                    pool.wait_ge(pool_step, 5)
                    pool.affine_select(out=mask_sb[:], in_=mask_sb[:], compare_op=ALU.is_ge, fill=NEG,
                                       base=-(D - 1), pattern=[[1, D]], channel_multiplier=1).then_inc(pool_step, 1)
                    pool.affine_select(out=ident[:], in_=ident[:], compare_op=ALU.not_equal, fill=1.0, base=0,
                                       pattern=[[-1, P]], channel_multiplier=1)
                    pool.affine_select(out=tri[:], in_=tri[:], compare_op=ALU.is_gt, fill=0.0, base=0,
                                       pattern=[[1, P]], channel_multiplier=-1)
                    pool.iota(iota_e[:], pattern=[[1, NE]], base=0, channel_multiplier=0,
                              allow_small_or_imprecise_dtypes=True)
                    pool.iota(tile_id[:], pattern=[[P, 6]], base=0, channel_multiplier=1,
                              allow_small_or_imprecise_dtypes=True).then_inc(pool_step, 1)

                @block.vector
                def _(dve):
                    dve.memset(zero[:], 0.0).then_inc(zeroed, 1)
                    dve.memset(wsel[:], 0.0).then_inc(zeroed, 1)
                    dve.memset(carry[:], 0.0)
                    dve.wait_ge(loaded, 16 * 15)
                    dve.wait_ge(blockmask_ready, 1)
                    dve.wait_ge(zeroed, 2)
                    for ty in range(2):
                        for h in range(HH):
                            last = dve.tensor_scalar(bd[:, ty, h * E:(h + 1) * E], wst[:, ty, :], bm[:, h:h + 1],
                                                     None, ALU.mult)
                        last.then_inc(bd_ready, 1)
                        for q in range(4):
                            dve.tensor_scalar(wsel[:, ty, q, HH * q:HH * (q + 1)], bm[:], wcol[:, ty:ty + 1],
                                              None, ALU.mult)
                    dve.tensor_scalar(hbout[:], bout_sb[:], 0.5, None, ALU.mult)
                    dve.wait_ge(w1_done, 1)
                    for i in range(2 * HG):
                        dve.tensor_copy(w1[:, i, :], psw[:, i, 0:P])
                    dve.tensor_copy(rpos[:], psw[:, 4, 0:D])

                @block.tensor
                def _(pe):
                    pe.wait_ge(loaded, 16 * 15)
                    for ty in range(2):
                        pe.wait_ge(bd_ready, ty + 1)
                        for g in range(HG):
                            pe.matmul(psw[:, ty * HG + g, 0:P], wdT[:, g, :], bd[:, ty, :], start=True, stop=True)
                    pe.matmul(psw[:, 4, 0:D], wpos_sb[:], rel_sb[:], start=True, stop=True).then_inc(w1_done, 1)

        with ExitStack() as c:
            xin = sb("xin", [P, 2, J, C], F32, c)
            xn = sb("xn", [P, J, C], F32, c)
            xT = sb("xT", [P, TC], F32, c)
            st6 = sb("st6", [P, J, 6], F32, c)
            mv = sb("mv", [P, J, 2], F32, c)
            ve = sb("ve", [P, J], F32, c)
            rstd = sb("rstd", [P, J], F32, c)
            s_sb = sb("s_sb", [P, 2 * HG, TC], F32, c)
            v_sb = sb("v_sb", [P, J, C], F32, c)
            probs = sb("probs", [P, J, NE], F32, c)
            sig_h = sb("sig_h", [I, TC], F32, c)
            act_h = sb("act_h", [I, TC], F32, c)
            part_sb = sb("part_sb", [P, J, C], F32, c)
            top = sb("top", [P, J, TOPK], F32, c)
            topi = sb("topi", [P, J, TOPK], U32, c)
            left = sb("left", [P, J, NE], F32, c)
            chosen = sb("chosen", [P, J, NE], BF16, c)
            gsum = sb("gsum", [P, J], F32, c)
            ginv = sb("ginv", [P, J], F32, c)
            rank_sb = sb("rank_sb", [P, J, NE], F32, c)
            ps_t = c.enter_context(nc.psum_tensor("ps_t", [P, TC], F32))
            ps_s = c.enter_context(nc.psum_tensor("ps_s", [P, 2, TC], F32))
            ps_v = c.enter_context(nc.psum_tensor("ps_v", [P, J, C], F32))
            ps_r = c.enter_context(nc.psum_tensor("ps_r", [P, 2, 512], F32))
            ps_h = c.enter_context(nc.psum_tensor("ps_h", [P, TC], F32))
            ps_y = c.enter_context(nc.psum_tensor("ps_y", [P, J, C], F32))
            x_loaded = [sem(f"x_loaded{u}") for u in range(2)]
            x_free = [sem(f"x_free{u}") for u in range(2)]
            var_ready, rstd_ready, xn_ready = sem("var_ready"), sem("rstd_ready"), sem("xn_ready")
            stats_ready = sem("stats_ready")
            xt_done, xt_copied = sem("xt_done"), sem("xt_copied")
            s_done, s_evac_act, s_evac_dve = sem("s_done"), sem("s_evac_act"), sem("s_evac_dve")
            v_done, v_evac = sem("v_done"), sem("v_evac")
            r_done, logits_ready, probs_ready = sem("r_done"), sem("logits_ready"), sem("probs_ready")
            h_done, sig_ready, acth_ready, y_done = sem("h_done"), sem("sig_ready"), sem("acth_ready"), sem("y_done")
            part_ready, top_step, chosen_ready = sem("part_ready"), sem("top_step"), sem("chosen_ready")
            rank_done, rank_ready, carry_used = sem("rank_done"), sem("rank_ready"), sem("carry_used")
            stored = {n: sem(f"stored_{n}") for n in ("xn", "s", "v", "part", "rank")}

            def rank_ps(j):
                return ps_r[:, j // 2, (j % 2) * NE:(j % 2 + 1) * NE]

            with nc.Block() as block:
                @block.sync
                def _(sp):
                    def body(k):
                        for u in range(2):
                            it = k * 2 + u
                            after(sp, x_free[u], k)
                            sp.dma_start(xin[:, u], chunk_rows(x_rows, it)).then_inc(x_loaded[u], 16)
                            after(sp, xn_ready, J * it + J)
                            sp.dma_start(chunk_rows(xn_dram, it), xn[:]).then_inc(stored["xn"], 16)
                            after(sp, part_ready, it + 1)
                            sp.dma_start(chunk_rows(part_dram, it), part_sb[:]).then_inc(stored["part"], 16)
                    peeled(sp, NCH // 2, body)
                    for s in stored.values():
                        sp.wait_ge(s, 16 * NCH)

                @block.gpsimd
                def _(pool):
                    def chunk(b, tc, it):
                        after(pool, var_ready, it + 1)
                        pool.tensor_tensor(rstd[:], ve[:], mhalf[:], ALU.pow).then_inc(rstd_ready, 1)
                        after(pool, s_evac_act, 2 * it + 2)
                        after(pool, s_evac_dve, 2 * it + 2)
                        pool.dma_start(s_dram[:, bass.ds(b, 1), :, bass.ds(tc * TC + PAD, TC)]
                                       .rearrange("i b p t -> p (i b) t"), s_sb[:]).then_inc(stored["s"], 16)
                        after(pool, v_evac, it + 1)
                        pool.dma_start(val_dram[bass.ds(b, 1), bass.ds(tc * TC + PAD, TC), :]
                                       .rearrange("b (j p) c -> p (b j) c", p=P), v_sb[:]).then_inc(stored["v"], 16)
                        after(pool, rank_ready, it + 1)
                        pool.dma_start(chunk_rows(rank_dram, it), rank_sb[:]).then_inc(stored["rank"], 16)

                    for tc in range(CB):
                        chunk(0, tc, tc)
                    with pool.Fori(1, B) as b:
                        with pool.Fori(0, CB) as tc:
                            chunk(b, tc, b * CB + tc)

                @block.scalar
                def _(act):
                    def body(it):
                        after(act, xt_done, it + 1)
                        act.activation(xT[:], ps_t[:], ACT.Copy).then_inc(xt_copied, 1)
                        after(act, stored["s"], 16 * it)
                        for i in (0, 2):
                            after(act, s_done, 4 * it + i + 1)
                            act.activation(s_sb[:, i, :], ps_s[:, 0, :], ACT.Copy).then_inc(s_evac_act, 1)
                        after(act, logits_ready, it + 1)
                        act.activation(probs[:], probs[:], ACT.Sigmoid).then_inc(probs_ready, 1)
                        after(act, h_done, it + 1)
                        act.activation(sig_h[:], ps_h[0:I, :], ACT.Sigmoid).then_inc(sig_ready, 1)
                    peeled(act, NCH, body)
                @block.tensor
                def _(pe):
                    def body(it):
                        after(pe, rank_ready, it)
                        for j in range(J):
                            after(pe, xn_ready, J * it + j + 1)
                            last = pe.transpose(ps_t[:, j * P:(j + 1) * P], xn[:, j, :], ident[:])
                        last.then_inc(xt_done, 1)
                        after(pe, xt_copied, it + 1)
                        for j in range(J):
                            last = pe.matmul(rank_ps(j), xT[:, j * P:(j + 1) * P], wr_sb[:], start=True, stop=True)
                        last.then_inc(r_done, 1)
                        after(pe, acth_ready, it)
                        pe.matmul(ps_h[0:I, :], wgs_sb[:], xT[:], start=True, stop=True).then_inc(h_done, 1)
                        for i in range(4):
                            after(pe, (s_evac_act, s_evac_dve)[i % 2], 2 * it + i // 2)
                            pe.matmul(ps_s[:, i % 2, :], w1[:, i, :], xT[:], start=True, stop=True).then_inc(s_done, 1)
                        after(pe, v_evac, it)
                        for j in range(J):
                            last = pe.matmul(ps_v[:, j, :], xT[:, j * P:(j + 1) * P], wval_sb[:], start=True, stop=True)
                        last.then_inc(v_done, 1)
                        after(pe, acth_ready, it + 1)
                        after(pe, part_ready, it)
                        for j in range(J):
                            last = pe.matmul(ps_y[:, j, :], act_h[:, j * P:(j + 1) * P], wds_sb[:], start=True, stop=True)
                        last.then_inc(y_done, 1)
                        after(pe, chosen_ready, it + 1)
                        for j in range(J):
                            for i in range(j + 1):
                                pe.matmul(rank_ps(j), tri[:] if i == j else ones[:], chosen[:, i, :],
                                          start=(i == 0), stop=(i == j))
                        for j in range(J):
                            last = pe.matmul(ps_t[:, 0:NE], ones[:], chosen[:, j, :], start=(j == 0), stop=(j == J - 1))
                        last.then_inc(rank_done, 1)
                    peeled(pe, NCH, body)
                @block.vector
                def _(dve):
                    def body(k):
                        for u in range(2):
                            it = k * 2 + u
                            after(dve, x_loaded[u], 16 * k + 16)
                            for j in range(J):
                                dve.bn_stats(st6[:, j, :], xin[:, u, j, :]).then_inc(stats_ready, 1)
                            hold(dve, stats_ready, 2 * J * it + J)
                            for j in range(J):
                                dve.bn_aggr(mv[:, j, :], st6[:, j, :]).then_inc(stats_ready, 1)
                            after(dve, stats_ready, 2 * J * it + 2 * J)
                            dve.tensor_scalar(ve[:], mv[:, :, 1], LN_EPS, None, ALU.add).then_inc(var_ready, 1)
                            after(dve, rstd_ready, it + 1)
                            after(dve, stored["xn"], 16 * it)
                            for j in range(J):
                                dve.tensor_scalar(xn[:, j, :], xin[:, u, j, :], mv[:, j, 0:1], rstd[:, j:j + 1],
                                                  ALU.subtract, ALU.mult).then_inc(xn_ready, 1)
                            after(dve, r_done, it + 1)
                            dve.tensor_tensor(probs[:].rearrange("p (a b) e -> p a b e", a=2),
                                              ps_r[:, :, 0:2 * NE].rearrange("p a (b e) -> p a b e", b=2),
                                              bias_sb[:].unsqueeze(1).unsqueeze(1).to_broadcast([P, 2, 2, NE]),
                                              ALU.add).then_inc(logits_ready, 1)
                            after(dve, stored["s"], 16 * it)
                            for i in (1, 3):
                                after(dve, s_done, 4 * it + i + 1)
                                dve.tensor_copy(s_sb[:, i, :], ps_s[:, 1, :]).then_inc(s_evac_dve, 1)
                            after(dve, sig_ready, it + 1)
                            dve.tensor_tensor(act_h[:], sig_h[:], ps_h[0:I, :], ALU.mult).then_inc(acth_ready, 1)
                            after(dve, v_done, it + 1)
                            after(dve, stored["v"], 16 * it)
                            dve.tensor_copy(v_sb[:], ps_v[:]).then_inc(v_evac, 1)
                            hold(dve, probs_ready, it + 1)
                            for j in range(J):
                                dve.max(top[:, j, :], probs[:, j, :]).then_inc(top_step, 1)
                            hold(dve, top_step, 4 * J * it + J)
                            for j in range(J):
                                dve.max_index(topi[:, j, :], top[:, j, :], probs[:, j, :]).then_inc(top_step, 1)
                            for j in range(J):
                                dve.match_replace(left[:, j, :], top[:, j, :], probs[:, j, :], -1.0).then_inc(top_step, 1)
                            after(dve, top_step, 4 * J * it + 3 * J)
                            dve.tensor_scalar(chosen[:], left[:], 0.0, None, ALU.is_lt).then_inc(chosen_ready, 1)
                            dve.tensor_reduce(gsum[:], top[:], AX.X, ALU.add).then_inc(top_step, 1)
                            after(dve, top_step, 4 * J * it + 3 * J + 1)
                            dve.tensor_scalar(gsum[:], gsum[:], GATE_EPS, None, ALU.add).then_inc(top_step, 1)
                            after(dve, top_step, 4 * J * it + 3 * J + 2)
                            dve.reciprocal(ginv[:], gsum[:]).then_inc(top_step, 1)
                            dve.tensor_copy(expert_all[:, bass.ds(it * J * TOPK, J * TOPK)],
                                            topi[:].rearrange("p j k -> p (j k)"))
                            after(dve, top_step, 4 * J * it + 3 * J + 3)
                            dve.tensor_tensor(top[:], top[:], ginv[:].unsqueeze(2).to_broadcast([P, J, TOPK]),
                                              ALU.mult).then_inc(top_step, 1)
                            after(dve, top_step, 4 * J * it + 3 * J + 4)
                            dve.tensor_scalar(gates_all[:, bass.ds(it * J * TOPK, J * TOPK)],
                                              top[:].rearrange("p j k -> p (j k)"), ROUTED_SCALE, None, ALU.mult)
                            after(dve, y_done, it + 1)
                            after(dve, stored["part"], 16 * it)
                            dve.tensor_tensor(part_sb[:], ps_y[:], xin[:, u], ALU.add).then_inc(part_ready, 1)
                            after(dve, part_ready, it + 1)
                            dve.sem_inc(x_free[u], 1)
                            after(dve, rank_done, it + 1)
                            after(dve, stored["rank"], 16 * it)
                            dve.tensor_tensor(rank_sb[:].rearrange("p (a b) e -> p a b e", a=2),
                                              ps_r[:, :, 0:2 * NE].rearrange("p a (b e) -> p a b e", b=2),
                                              carry[:].unsqueeze(1).unsqueeze(1).to_broadcast([P, 2, 2, NE]), ALU.add)\
                                .then_inc(carry_used, 1)
                            after(dve, carry_used, it + 1)
                            dve.tensor_tensor(carry[:], carry[:], ps_t[:, 0:NE], ALU.add).then_inc(rank_ready, 1)
                            after(dve, rank_ready, it + 1)
                    peeled(dve, NCH // 2, body)
        with ExitStack() as c:
            ci = sb("ci", [P, NE], I32, c)
            ntl = sb("ntl", [P, NE], F32, c)
            cum = [sb(f"cum{i}", [P, NE], F32, c) for i in range(2)]
            le = sb("le", [P, 6, NE], F32, c)
            tef = sb("tef", [P, 6], F32, c)
            tei = sb("tei", [P, 6], I32, c)
            place_step, tiles_known = sem("place_step"), sem("tiles_known")
            te_stored = sem("te_stored")
            with nc.Block() as block:
                @block.vector
                def _(dve):
                    n = 0

                    def then(ins):
                        nonlocal n
                        n += 1
                        ins.then_inc(place_step, 1)
                        after(dve, place_step, n)

                    then(dve.tensor_scalar(ci[:], carry[:], float(P - 1), None, ALU.add))
                    then(dve.tensor_scalar(ci[:], ci[:], 7, None, ALU.logical_shift_right))
                    then(dve.tensor_copy(ntl[:], ci[:]))
                    src, s = ntl, 1
                    i = 0
                    while s < NE:
                        dst = cum[i % 2]
                        dve.tensor_copy(dst[:, 0:s], src[:, 0:s])
                        then(dve.tensor_tensor(dst[:, s:NE], src[:, s:NE], src[:, 0:NE - s], ALU.add))
                        src, s, i = dst, 2 * s, i + 1
                    for g in range(6):
                        last = dve.tensor_scalar(le[:, g, :], src[:], tile_id[:, g:g + 1], None, ALU.is_le)
                    then(last)
                    then(dve.tensor_reduce(tef[:], le[:], AX.X, ALU.add))
                    then(dve.tensor_scalar(tei[:], tef[:], float(NE - 1), None, ALU.min))
                    dve.sem_inc(tiles_known, 1)
                    then(dve.tensor_tensor(carry[:], src[:], ntl[:], ALU.subtract))
                    then(dve.tensor_scalar(carry[:], carry[:], float(P), None, ALU.mult))

                @block.sync
                def _(sp):
                    sp.wait_ge(tiles_known, 1)
                    sp.dma_start(tile_expert_dram.rearrange("o (g p) -> p (o g)", p=P), tei[:], allow_slow_non_contiguous=True)\
                        .then_inc(te_stored, 16)
                    sp.wait_ge(te_stored, 16)

        with ExitStack() as c:
            xr = sb("xr", [P, J, C], F32, c)
            rk = sb("rk", [P, J, NE], F32, c)
            ex = sb("ex", [P, J * TOPK], F32, c)
            pick = sb("pick", [P, J * TOPK, NE], F32, c)
            slotf = sb("slotf", [P, J * TOPK], F32, c)
            sloti = sb("sloti", [P, J * TOPK], U32, c)
            rows_in, ranks_in = sem("rows_in"), sem("ranks_in")
            slot_step, slots_ready, scattered = sem("slot_step"), sem("slots_ready"), sem("scattered")
            NS = J * TOPK
            with nc.Block() as block:
                @block.sync
                def _(sp):
                    def body(it):
                        after(sp, slots_ready, it)
                        sp.dma_start(rk[:], chunk_rows(rank_dram, it)).then_inc(ranks_in, 16)
                        after(sp, scattered, 16 * NS * it)
                        sp.dma_start(xr[:], chunk_rows(xn_dram, it)).then_inc(rows_in, 16)
                    peeled(sp, NCH, body)
                @block.vector
                def _(dve):
                    def body(it):
                        after(dve, ranks_in, 16 * it + 16)
                        dve.tensor_tensor(rk[:], rk[:], carry[:].unsqueeze(1).to_broadcast([P, J, NE]),
                                          ALU.add).then_inc(slot_step, 1)
                        dve.tensor_copy(ex[:], expert_all[:, bass.ds(it * NS, NS)]).then_inc(slot_step, 1)
                        after(dve, slot_step, (2 + NS) * it + 2)
                        for n in range(NS):
                            dve.scalar_tensor_tensor(out=pick[:, n, :], in0=iota_e[:], scalar=ex[:, n:n + 1],
                                                     in1=rk[:, n // TOPK, :], op0=ALU.is_equal, op1=ALU.mult,
                                                     accum_out=slotf[:, n:n + 1]).then_inc(slot_step, 1)
                        after(dve, slot_step, (2 + NS) * it + 2 + NS)
                        after(dve, scattered, 16 * NS * it)
                        dve.tensor_copy(slots_all[:, bass.ds(it * NS, NS)], slotf[:])
                        dve.tensor_copy(sloti[:], slotf[:]).then_inc(slots_ready, 1)
                    peeled(dve, NCH, body)
                @block.gpsimd
                def _(pool):
                    def body(it):
                        after(pool, rows_in, 16 * it + 16)
                        hold(pool, slots_ready, it + 1)
                        for n in range(NS):
                            pool.indirect_dma_start(xslot_dram, bass.IndirectOffsetOnAxis(ap=sloti[:, n:n + 1], axis=0),
                                                    xr[:, n // TOPK, :], None).then_inc(scattered, 16)
                    peeled(pool, NCH, body)
                    pool.wait_ge(scattered, 16 * NS * NCH)

        with ExitStack() as c:
            NI = 16
            CH = 4
            u_dve = sb("u_dve", [P, 3, 8, TC], F32, c)
            u_pool = sb("u_pool", [P, 2, 8, TC], F32, c)
            s_win = sb("s_win", [P, HG, 2, SW], F32, c)
            tanh_sb = sb("tanh_sb", [P, 2, TC], F32, c)
            lg = sb("lg", [P, 2, CH, TC], F32, c)
            ml = sb("ml", [P, J, D, HH], F32, c)
            mx = sb("mx", [P, J, HH], F32, c)
            wsum = sb("wsum", [P, J, HH], F32, c)
            winv = sb("winv", [P, J, HH], F32, c)
            band = sb("band", [P, J, BANDW], F32, c)
            at_sb = sb("at_sb", [P, 2, 4, P], F32, c)
            v_raw = sb("v_raw", [P, 2 * J, C], F32, c)
            v_msk = sb("v_msk", [P, 2 * J, H * 32], F32, c)
            mask_t = sb("mask_t", [P, D], F32, c)
            oT_sb = sb("oT_sb", [P, TC], F32, c)
            part_t = sb("part_t", [P, J, C], F32, c)
            y_sb = sb("y_sb", [P, J, C], F32, c)
            ps_l = c.enter_context(nc.psum_tensor("ps_l", [P, 2, 2, TC], F32))
            ps_p = c.enter_context(nc.psum_tensor("ps_p", [P, D, HH], F32))
            ps_a = c.enter_context(nc.psum_tensor("ps_a", [P, 4, P], F32))
            ps_o = c.enter_context(nc.psum_tensor("ps_o", [P, TC], F32))
            ps_c = c.enter_context(nc.psum_tensor("ps_c", [P, J, C], F32))
            win_loaded = [sem(f"win_loaded{g}") for g in range(HG)]
            sub_dve, sub_pool, gelu_done, item_done = sem("sub_dve"), sem("sub_pool"), sem("gelu_done"), sem("item_done")
            tanh_done, logits_in = sem("tanh_done"), sem("logits_in")
            turned, max_in, centred, exped = sem("turned"), sem("max_in"), sem("centred"), sem("exped")
            masked, sum_in, inv_in, normed = sem("masked"), sem("sum_in"), sem("inv_in"), sem("normed")
            band_out, band_in, band_turned, band_copied = sem("band_out"), sem("band_in"), sem("band_turned"), sem("band_copied")
            av_done, v_loaded, v_spread = sem("av_done"), sem("v_loaded"), sem("v_spread")
            mask_loaded, part_loaded = sem("mask_loaded"), sem("part_loaded")
            o_copied, cproj_done, y_ready, y_stored = sem("o_copied"), sem("cproj_done"), sem("y_ready"), sem("y_stored")
            v_zeroed = sem("v_zeroed")
            NSTEP = 2 * NCH

            def steps(e, step):
                step(0, 0, 0, True, False, False)
                step(1, 0, 1, True, True, False)
                step(2, 1, 0, True, True, True)
                step(3, 1, 1, True, True, True)
                with e.Fori(2, NCH) as it:
                    for par in range(2):
                        step(it * 2 + par, it, par, True, True, True)
                step(NSTEP, NCH, 0, False, True, True)
                step(NSTEP + 1, NCH, 1, False, False, True)

            def offsets(n):
                return n // 4, 16 * (n // 4) + 8 * (n % 4 // 2), n % 2

            def windows(par, ty, d0, nd):
                row = s_win[:, par, ty, d0 + 1:d0 + 1 + TC]
                return bass.AP(row.tensor, row.offset, [list(row.ap[0]), [1, nd], [1, TC]])

            with nc.Block() as block:
                @block.sync
                def _(sp):
                    def load_windows(b, tc, it, par):
                        hold(sp, sub_dve, 12 * (2 * it + par - 1) if not isinstance(it, int) or it > 0 else 0)
                        after(sp, sub_pool, 4 * (2 * it + par - 1) if not isinstance(it, int) or it > 0 else 0)
                        for ty in range(2):
                            sp.dma_start(s_win[:, par, ty, :],
                                         s_dram[ty * HG + par, bass.ds(b, 1), :, bass.ds(tc * TC, SW)]
                                         .rearrange("b p t -> p (b t)")).then_inc(win_loaded[par], 16)

                    def load_chunk(b, tc, it):
                        after(sp, masked, 2 * it)
                        sp.dma_start(mask_t[:], mask_dram[bass.ds(tc, 1)].rearrange("n p d -> p (n d)"))\
                            .then_inc(mask_loaded, 16)
                        after(sp, v_spread, it)
                        for s in range(2 * J):
                            sp.dma_start(v_raw[:, s, :],
                                         val_dram[bass.ds(b, 1), bass.ds(tc * TC + s * HALF + 1, P), :]
                                         .rearrange("b p c -> p (b c)")).then_inc(v_loaded, 16)

                    def band_trip(u):
                        after(sp, normed, u + 1)
                        for h in range(2):
                            first = band_dram[0, :, h * HALF:(h + 1) * HALF, :]
                            skewed = bass.AP(first.tensor, first.offset,
                                             [[BANDW + HH, HALF], [P * BANDW, J], [1, D * HH]])
                            sp.dma_start(skewed, ml[h * HALF:(h + 1) * HALF].rearrange("p j d h -> p j (d h)"))\
                                .then_inc(band_out, 16)
                        hold(sp, band_out, 32 * u + 32)
                        after(sp, band_turned, 8 * u)
                        sp.dma_start(band[:], band_dram[0].rearrange("j p f -> p j f")).then_inc(band_in, 16)

                    load_windows(0, 0, 0, 0)
                    load_windows(0, 0, 0, 1)
                    load_chunk(0, 0, 0)

                    def store_y(it):
                        after(sp, y_ready, it + 1)
                        sp.dma_start(chunk_rows(attn_dram, it), y_sb[:]).then_inc(y_stored, 16)

                    def load_part(it):
                        after(sp, y_ready, it)
                        sp.dma_start(part_t[:], chunk_rows(part_dram, it)).then_inc(part_loaded, 16)

                    def chunk(b, tc, it, first=False):
                        load_windows(b, tc, it, 0)
                        band_trip(2 * it - 1)
                        load_windows(b, tc, it, 1)
                        load_chunk(b, tc, it)
                        load_part(it - 1)
                        band_trip(2 * it)
                        store_y(it - 1)

                    band_trip(0)
                    for tc in range(1, CB):
                        chunk(0, tc, tc)
                    with sp.Fori(1, B) as b:
                        with sp.Fori(0, CB) as tc:
                            chunk(b, tc, b * CB + tc)
                    band_trip(NSTEP - 1)
                    load_part(NCH - 1)
                    store_y(NCH - 1)
                    sp.wait_ge(y_stored, 16 * NCH)

                @block.gpsimd
                def _(pool):
                    pool.memset(v_msk[:], 0.0).then_inc(v_zeroed, 1)
                    pool.wait_ge(v_zeroed, 1)

                    def spread(it):
                        after(pool, v_loaded, 16 * 2 * J * (it + 1))
                        hold(pool, av_done, 16 * it)
                        for s in range(2 * J):
                            dst = v_msk[:, s, 0:HS]
                            last = pool.tensor_copy(
                                bass.AP(dst.tensor, dst.offset, [list(dst.ap[0]), [4 * 32, H // 4], [32 + HS, 4], [1, HS]]),
                                v_raw[:, s, :].rearrange("p (g i e) -> p g i e", g=H // 4, i=4))
                        last.then_inc(v_spread, 1)

                    def step(s, it, par, items, soft, av):
                        for n in range(NI):
                            cgrp, d0, ty = offsets(n)
                            if items and n % 4 == 3:
                                if n == 3:
                                    after(pool, win_loaded[par], 32 * it + 32)
                                after(pool, item_done, NI * s + n - 7)
                                pool.tensor_tensor(
                                    u_pool[:, cgrp % 2], windows(par, ty, d0, 8),
                                    s_win[:, par, ty, PAD:PAD + TC].unsqueeze(1).to_broadcast([P, 8, TC]),
                                    ALU.subtract).then_inc(sub_pool, 1)
                            if soft and n == 11:
                                after(pool, inv_in, s)
                                pool.tensor_tensor(ml[:].rearrange("p j d h -> p j d h"), ml[:],
                                                   winv[:].unsqueeze(2).to_broadcast([P, J, D, HH]),
                                                   ALU.mult).then_inc(normed, 1)
                            if par == 1 and n == 15 and items:
                                spread(it)

                    steps(pool, step)

                @block.scalar
                def _(act):
                    def step(s, it, par, items, soft, av):
                        for n in range(NI):
                            cgrp, d0, ty = offsets(n)
                            if items:
                                if n % 4 == 3:
                                    after(act, sub_pool, 4 * s + cgrp + 1)
                                    u = u_pool[:, cgrp % 2]
                                else:
                                    after(act, sub_dve, 12 * s + 3 * cgrp + n % 4 + 1)
                                    u = u_dve[:, n % 4]
                                if ty:
                                    act.activation(u, u, ACT.Gelu, bias=bdmg_sb[:]).then_inc(gelu_done, 1)
                                else:
                                    act.activation(u, u, ACT.Gelu).then_inc(gelu_done, 1)
                            if n % 4 == 1 and (items if n > 1 else soft):
                                done = NI * s + n - 1
                                act.wait_ge(item_done, done)
                                k = 4 * s + cgrp - 1
                                after(act, logits_in, k - 1)
                                act.activation(tanh_sb[:, (cgrp - 1) % 2], ps_l[:, (cgrp - 1) % 2, 1], ACT.Tanh,
                                               bias=hbout[:], scale=0.5).then_inc(tanh_done, 1)
                            if n == 8 and soft:
                                after(act, centred, 4 * s)
                                act.activation(ml[:], ml[:], ACT.Exp).then_inc(exped, 1)
                            if n == 10 and av and par == 1:
                                after(act, av_done, 8 * (s - 1))
                                act.activation(oT_sb[:], ps_o[:], ACT.Copy).then_inc(o_copied, 1)

                    steps(act, step)

                @block.vector
                def _(dve):
                    def step(s, it, par, items, soft, av):
                        for n in range(NI):
                            cgrp, d0, ty = offsets(n)
                            if items and n % 4 != 3:
                                if n == 0:
                                    after(dve, win_loaded[par], 32 * it + 32)
                                after(dve, item_done, NI * s + n - 3)
                                here = s_win[:, par, ty, PAD:PAD + TC]
                                if ty:
                                    last = dve.tensor_tensor(u_dve[:, n % 4], windows(par, ty, d0, 8),
                                                             here.unsqueeze(1).to_broadcast([P, 8, TC]), ALU.subtract)
                                else:
                                    for d in range(8):
                                        last = dve.scalar_tensor_tensor(
                                            out=u_dve[:, n % 4, d, :], in0=s_win[:, par, ty, d0 + d + 1:d0 + d + 1 + TC],
                                            scalar=rpos[:, d0 + d:d0 + d + 1], in1=here, op0=ALU.add, op1=ALU.subtract)
                                last.then_inc(sub_dve, 1)
                            if n % 4 == 2 and (items if n > 2 else soft):
                                k = 4 * s + cgrp - 1
                                after(dve, tanh_done, k + 1)
                                pu = par if n > 2 else 1 - par
                                if n > 2:
                                    after(dve, turned, 4 * (s - 1))
                                dve.scalar_tensor_tensor(out=lg[:, pu, (cgrp - 1) % 4, :], in0=tanh_sb[:, (cgrp - 1) % 2],
                                                         scalar=-5.0, in1=ps_l[:, (cgrp - 1) % 2, 0], op0=ALU.mult,
                                                         op1=ALU.add).then_inc(logits_in, 1)
                            if soft and 4 <= n <= 7:
                                j = n - 4
                                after(dve, turned, 4 * (s - 1) + j + 1)
                                if j == 0:
                                    after(dve, mask_loaded, 16 * ((it if par else it - 1) + 1))
                                    after(dve, band_out, 32 * (s - 1))
                                    dve.tensor_tensor(ml[:, 0], ps_p[:],
                                                      mask_t[:].unsqueeze(2).to_broadcast([P, D, HH]), ALU.add)\
                                        .then_inc(masked, 1)
                                    after(dve, masked, s)
                                src = ml[:, 0] if j == 0 else ps_p[:]
                                dve.tensor_reduce(mx[:, j, :], src.rearrange("p d h -> p h d"), AX.X, ALU.max)\
                                    .then_inc(max_in, 1)
                                after(dve, max_in, 4 * (s - 1) + j + 1)
                                dve.tensor_tensor(ml[:, j], src, mx[:, j, :].unsqueeze(1).to_broadcast([P, D, HH]),
                                                  ALU.subtract).then_inc(centred, 1)
                            if soft and n == 10:
                                after(dve, exped, s)
                                dve.tensor_reduce(wsum[:], ml[:].rearrange("p j d h -> p j h d"), AX.X, ALU.add)\
                                    .then_inc(sum_in, 1)
                                after(dve, sum_in, s)
                                dve.reciprocal(winv[:], wsum[:]).then_inc(inv_in, 1)
                            if av and n <= 7:
                                k = 8 * (s - 2) + n
                                after(dve, band_turned, k + 1)
                                after(dve, av_done, k - 1 if n else k)
                                dve.tensor_copy(at_sb[:, n % 2], ps_a[:]).then_inc(band_copied, 1)
                            if av and par == 1 and n == 12:
                                after(dve, cproj_done, it)
                                after(dve, part_loaded, 16 * it)
                                after(dve, y_stored, 16 * (it - 1))
                                dve.tensor_tensor(y_sb[:], ps_c[:], part_t[:], ALU.add).then_inc(y_ready, 1)

                    steps(dve, step)

                @block.tensor
                def _(pe):
                    def step(s, it, par, items, soft, av):
                        for n in range(NI + 1):
                            cgrp, d0, ty = offsets(n)
                            if items and n < NI:
                                if n % 4 < 2:
                                    after(pe, logits_in, 4 * s + cgrp - 1)
                                after(pe, gelu_done, NI * s + n + 1)
                                u = u_pool[:, cgrp % 2] if n % 4 == 3 else u_dve[:, n % 4]
                                for d in range(8):
                                    q, g = (d0 + d) % 16 // 4, d % 4
                                    last = pe.matmul(ps_l[32 * g:32 * g + 32, cgrp % 2, ty, :], wsel[:, ty, q, :],
                                                     u[:, d, :], start=(q == 0), stop=(q == 3))
                                last.then_inc(item_done, 1)
                            if av and n <= 7:
                                k = 8 * (s - 2) + n
                                if n == 0:
                                    after(pe, band_in, 16 * (s - 1))
                                after(pe, band_copied, k)
                                for i in range(4):
                                    last = pe.transpose(ps_a[:, i, :], band[:, n // 2, 4 * (n % 2) + i:BANDW:HH], ident[:])
                                last.then_inc(band_turned, 1)
                            if av and 1 <= n <= 8:
                                k = n - 1
                                j, hh = k // 2, k % 2
                                if k == 0:
                                    after(pe, v_spread, it)
                                    if par == 0:
                                        after(pe, o_copied, it - 1)
                                after(pe, band_copied, 8 * (s - 2) + k + 1)
                                g = 2 * par + hh
                                for half in range(2):
                                    for i in range(4):
                                        h = 4 * g + i
                                        last = pe.matmul(
                                            ps_o[32 * g:32 * g + 32, j * P + half * HALF:j * P + (half + 1) * HALF],
                                            v_msk[:, 2 * j + half, 32 * h:32 * h + 32],
                                            at_sb[:, k % 2, i, half * HALF:(half + 1) * HALF],
                                            start=(i == 0), stop=(i == 3))
                                last.then_inc(av_done, 1)
                            if soft and 3 <= n <= 6:
                                j = n - 3
                                after(pe, logits_in, 4 * s)
                                after(pe, centred, 4 * (s - 1) + j)
                                for g in range(CH):
                                    last = pe.transpose(
                                        ps_p[:, 16 * g:16 * g + 16, :].rearrange("p (q g) h -> p g q h", g=4),
                                        lg[:, 1 - par, g, j * P:(j + 1) * P], ident[:])
                                last.then_inc(turned, 1)
                            if av and par == 1 and n == 11:
                                after(pe, o_copied, it)
                                after(pe, y_ready, it - 1)
                                for j in range(J):
                                    last = pe.matmul(ps_c[:, j, :], oT_sb[:, j * P:(j + 1) * P], wc_sb[:],
                                                     start=True, stop=True)
                                last.then_inc(cproj_done, 1)

                    steps(pe, step)

        with ExitStack() as c:
            te_sb = sb("te_sb", [1, 6 * P], I32, c)
            xs = sb("xs", [P, 2, TB, C], F32, c)
            we = sb("we", [P, 2, TB, P], F32, c)
            xsT = sb("xsT", [P, 2, TB * P], F32, c)
            sg = sb("sg", [P, 2, TB * P], F32, c)
            hs = sb("hs", [P, 2, TB * P], F32, c)
            ys = sb("ys", [P, 2, TB, C], F32, c)
            ps_x = c.enter_context(nc.psum_tensor("ps_x", [P, 2, 512], F32))
            ps_e = c.enter_context(nc.psum_tensor("ps_e", [P, 2, 512], F32))
            ps_z = c.enter_context(nc.psum_tensor("ps_z", [P, 2, 512], F32))
            te_in = sem("te_in")
            rows_loaded = [sem(f"rows_loaded{u}") for u in range(2)]
            experts_loaded = [sem(f"experts_loaded{u}") for u in range(2)]
            rows_turned, rows_copied, up_done, gate_done, hidden_done, down_done = (
                sem("rows_turned"), sem("rows_copied"), sem("up_done"), sem("gate_done"), sem("hidden_done"), sem("down_done"))
            down_by = [sem(f"down_by{u}") for u in range(2)]
            ys_ready = sem("ys_ready")
            ys_stored = [sem(f"ys_stored{u}") for u in range(2)]
            with nc.Block() as block:
                def slot_rows(t, n):
                    return t[bass.ds(n * TB * P, TB * P), :].rearrange("(i p) c -> p i c", p=P)

                @block.sync
                def _(sp):
                    sp.dma_start(te_sb[:], tile_expert_dram).then_inc(te_in, 16)
                    sp.wait_ge(te_in, 16)
                    def body(k):
                        for u in range(2):
                            after(sp, down_by[u], k)
                            sp.dma_start(xs[:, u], slot_rows(xslot_dram, k * 2 + u)).then_inc(rows_loaded[u], 16)
                            for i in range(TB):
                                e = sp.value_load(te_sb[0:1, bass.ds(k * 2 * TB + u * TB + i, 1)], min_val=0, max_val=NE - 1)
                                sp.dma_start(we[:, u, i, :], w_expert[bass.ds(e, 1)].rearrange("e p f -> p (e f)"))\
                                    .then_inc(experts_loaded[u], 16)
                    peeled(sp, NEST // 2, body)
                @block.tensor
                def _(pe):
                    def body(k):
                        for u in range(2):
                            n = k * 2 + u
                            after(pe, rows_loaded[u], 16 * k + 16)
                            for i in range(TB):
                                last = pe.transpose(ps_x[:, u, i * P:(i + 1) * P], xs[:, u, i, :], ident[:])
                            last.then_inc(rows_turned, 1)
                            after(pe, experts_loaded[u], 16 * TB * k + 16 * TB)
                            after(pe, rows_copied, n + 1)
                            for i in range(TB):
                                for half in range(2):
                                    last = pe.matmul(ps_e[half * I:(half + 1) * I, u, i * P:(i + 1) * P], we[:, u, i, 0:I],
                                                     xsT[:, u, i * P:(i + 1) * P], start=True, stop=True)
                            last.then_inc(up_done, 1)
                            after(pe, hidden_done, n + 1)
                            for i in range(TB):
                                for half in range(2):
                                    rows = slice(half * I, (half + 1) * I)
                                    last = pe.matmul(ps_z[:, half, i * I:(i + 1) * I],
                                                     hs[rows, u, i * P:(i + 1) * P], we[rows, u, i, I:2 * I],
                                                     start=True, stop=True)
                            last.then_inc(down_done, 1)
                            after(pe, ys_ready, n + 1)
                            pe.sem_inc(down_by[u], 1)
                    peeled(pe, NEST // 2, body)
                @block.scalar
                def _(act):
                    def body(k):
                        for u in range(2):
                            n = k * 2 + u
                            after(act, rows_turned, n + 1)
                            act.activation(xsT[:, u], ps_x[:, u, 0:TB * P], ACT.Copy).then_inc(rows_copied, 1)
                            after(act, up_done, n + 1)
                            act.activation(sg[:, u], ps_e[:, u, 0:TB * P], ACT.Sigmoid).then_inc(gate_done, 1)
                    peeled(act, NEST // 2, body)
                @block.vector
                def _(dve):
                    def body(k):
                        for u in range(2):
                            n = k * 2 + u
                            after(dve, gate_done, n + 1)
                            dve.tensor_tensor(hs[:, u], sg[:, u], ps_e[:, u, 0:TB * P], ALU.mult).then_inc(hidden_done, 1)
                            after(dve, down_done, n + 1)
                            after(dve, ys_stored[u], 16 * k)
                            dve.tensor_copy(ys[:, u].rearrange("p i (h c) -> p h i c", h=2),
                                            ps_z[:, :, 0:TB * I].rearrange("p h (i c) -> p h i c", i=TB))\
                                .then_inc(ys_ready, 1)
                    peeled(dve, NEST // 2, body)
                @block.gpsimd
                def _(pool):
                    def body(k):
                        for u in range(2):
                            n = k * 2 + u
                            after(pool, ys_ready, n + 1)
                            pool.dma_start(slot_rows(yslot_dram, n), ys[:, u]).then_inc(ys_stored[u], 16)
                    peeled(pool, NEST // 2, body)
                    for u in range(2):
                        pool.wait_ge(ys_stored[u], 16 * (NEST // 2))

        with ExitStack() as c:
            NS = J * TOPK
            yg = sb("yg", [P, NS, C], F32, c)
            si = sb("si", [P, NS], U32, c)
            gt = sb("gt", [P, NS], F32, c)
            acc = sb("acc", [P, 2, J, C], F32, c)
            base_in = [sem(f"base_in{u}") for u in range(2)]
            slots_here, gathered, summed, chain = sem("slots_here"), sem("gathered"), sem("summed"), sem("chain")
            out_stored = [sem(f"out_stored{u}") for u in range(2)]
            with nc.Block() as block:
                @block.sync
                def _(sp):
                    def body(k):
                        for u in range(2):
                            it = k * 2 + u
                            after(sp, out_stored[u], 16 * k)
                            sp.dma_start(acc[:, u], chunk_rows(attn_dram, it)).then_inc(base_in[u], 16)
                            after(sp, summed, it + 1)
                            sp.dma_start(chunk_rows(out_rows, it), acc[:, u]).then_inc(out_stored[u], 16)
                    peeled(sp, NCH // 2, body)
                    for u in range(2):
                        sp.wait_ge(out_stored[u], 16 * (NCH // 2))

                @block.gpsimd
                def _(pool):
                    def body(it):
                        hold(pool, slots_here, it + 1)
                        for n in range(NS):
                            pool.indirect_dma_start(yg[:, n, :], None, yslot_dram,
                                                    bass.IndirectOffsetOnAxis(ap=si[:, n:n + 1], axis=0))\
                                .then_inc(gathered, 16)
                    peeled(pool, NCH, body)
                @block.vector
                def _(dve):
                    def body(k):
                        for u in range(2):
                            it = k * 2 + u
                            dve.tensor_copy(gt[:], gates_all[:, bass.ds(it * NS, NS)]).then_inc(chain, 1)
                            dve.tensor_copy(si[:], slots_all[:, bass.ds(it * NS, NS)]).then_inc(slots_here, 1)
                            after(dve, base_in[u], 16 * k + 16)
                            after(dve, gathered, 16 * NS * it + 16 * NS)
                            after(dve, chain, (1 + TOPK) * it + 1)
                            for kk in range(TOPK):
                                for j in range(J):
                                    n = j * TOPK + kk
                                    last = dve.scalar_tensor_tensor(
                                        out=acc[:, u, j, :], in0=yg[:, n, :], scalar=gt[:, n:n + 1],
                                        in1=acc[:, u, j, :], op0=ALU.mult, op1=ALU.add)
                                last.then_inc(chain, 1)
                                after(dve, chain, (1 + TOPK) * it + 2 + kk)
                            dve.sem_inc(summed, 1)
                    peeled(dve, NCH // 2, body)
_OUT = ((8, 1024, 128), "float32")


def kernel(**inputs):
    import numpy as _np
    import concourse.bacc as _bacc
    from concourse import mybir as _mybir
    from concourse.bass_utils import run_bass_kernel_spmd as _run

    a = {k.replace("L0_", ""): _np.asarray(v) for k, v in inputs.items()}
    heads = 8
    wg = a["ffn_w_gate"].transpose(0, 2, 1)
    wd = a["ffn_w_down"].transpose(0, 2, 1)
    half = wd.shape[2] // 2
    wd = _np.concatenate([wd[:, :, :half], wd[:, :, half:]], axis=1)
    laid = {
        "x": a["attn_x"],
        "w_dispT": a["attn_W_disp"].T,
        "w_val": a["attn_W_val"],
        "relT": a["attn_rel_pos_emb"].T,
        "w_strain": _np.tile(a["attn_W_strain"], (heads, 1)),
        "w_pos": _np.tile(a["attn_W_pos"], (1, heads)),
        "w_bond": _np.tile(a["attn_W_bond"], (heads, 1)),
        "w_dmg": _np.tile(a["attn_W_dmg"], (heads, 1)),
        "b_dmg": _np.tile(a["attn_b_dmg"][:, None], (heads, 1)),
        "w_dmg_out": _np.tile(a["attn_W_dmg_out"], (heads, 1)),
        "b_dmg_out": _np.tile(a["attn_b_dmg_out"][:, None], (128, 1)),
        "w_cproj": a["attn_W_cproj"],
        "router_wT": a["ffn_router_w"].T,
        "expert_bias": a["ffn_expert_bias"],
        "w_expert": _np.concatenate([wg, wd], axis=2),
        "w_gate_sharedT": a["ffn_w_gate_shared"].T,
        "w_down_sharedT": a["ffn_w_down_shared"].T,
    }
    nc = _bacc.Bacc("TRN2", target_bir_lowering=False, num_devices=1)
    arrays, args = {}, []
    for name, v in laid.items():
        arrays[f"in_{name}"] = _np.ascontiguousarray(v)
        args.append(nc.dram_tensor(f"in_{name}", v.shape, _mybir.dt.from_np(v.dtype), kind="ExternalInput").ap())
    args.append(nc.dram_tensor("out_0", _OUT[0], _mybir.dt.from_np(_np.dtype(_OUT[1])), kind="ExternalOutput").ap())
    moe_attention_layer(nc, *args)
    r = _run(nc, [arrays], core_ids=[0])
    return r.results[0]["out_0"]
```

```python
from contextlib import ExitStack

import concourse.bass as bass
from concourse import mybir

F32 = mybir.dt.float32
BF16 = mybir.dt.bfloat16
I32 = mybir.dt.int32
U32 = mybir.dt.uint32
ALU = mybir.AluOpType
ACT = mybir.ActivationFunctionType
AX = mybir.AxisListType

P = 128
NEG = -1.0e30
LN_EPS = 1e-5
GATE_EPS = 1e-9
ROUTED_SCALE = 2.5
TOPK = 8
POOL_ITEMS = (3,)


def moe_attention_layer(nc, x, w_dispT, w_val, relT, w_strain, w_pos, w_bond, w_dmg, b_dmg,
                        w_dmg_out, b_dmg_out, w_cproj, router_wT, expert_bias, w_expert,
                        w_gate_sharedT, w_down_sharedT, out):
    B, T, C = x.shape
    D, E = relT.shape[1], relT.shape[0]
    H = w_dispT.shape[0] // E
    HS = C // H
    NE = router_wT.shape[1]
    I = w_gate_sharedT.shape[1]
    HG = 2
    HH = H // HG
    TC = 512
    CB = T // TC
    NCH = B * CB
    J = TC // P
    NBLK = NCH * J
    NTOK = B * T
    PAD = D
    SW = TC + PAD
    NTILE = NTOK * TOPK // P + NE
    NSLOT = NTILE * P
    TB = 4
    NBATCH = NTILE // TB
    BUF = 8
    BANDW = P * HH
    HALF = P // 2
    assert C == P and HH * E == P and D == HALF and NTILE % (BUF * TB) == 0

    with ExitStack() as ctx:
        def dram(name, shape, dt=F32):
            return nc.dram_tensor(name, shape, dt).ap()

        def sem(name):
            return ctx.enter_context(nc.semaphore(name))

        s_dram = dram("s_dram", (2 * HG, B, P, PAD + T))
        val_dram = dram("val_dram", (B, PAD + T + PAD, C))
        xn_dram = dram("xn_dram", (NTOK, C))
        rank_dram = dram("rank_dram", (NTOK, NE))
        part_dram = dram("part_dram", (NTOK, C))
        attn_dram = dram("attn_dram", (NTOK, C))
        band_dram = dram("band_dram", (2, J, P, BANDW))
        mask_dram = dram("mask_dram", (CB, P, D))
        tile_expert_dram = dram("tile_expert_dram", (1, 6 * P), I32)
        xslot_dram = dram("xslot_dram", (NSLOT, C))
        yslot_dram = dram("yslot_dram", (NSLOT, C))
        x_rows = x.rearrange("b t c -> (b t) c")
        out_rows = out.rearrange("b t c -> (b t) c")

        def chunk_rows(t, it):
            return t[bass.ds(it * TC, TC), :].rearrange("(j p) c -> p j c", p=P)

        held = sem("held")

        def some(n):
            return not isinstance(n, int) or n > 0

        def peeled(e, n, body):
            body(0)
            with e.Fori(1, n) as i:
                body(i)

        def sb(name, shape, dt=F32, c=ctx):
            return c.enter_context(nc.sbuf_tensor(name, shape, dt))

        ident = sb("ident", [P, P])
        gates_all = sb("gates_all", [P, NBLK * TOPK])
        expert_all = sb("expert_all", [P, NBLK * TOPK])
        slots_all = sb("slots_all", [P, NBLK * TOPK], U32)
        w1 = sb("w1", [P, 2 * HG, P])
        wval_sb = sb("wval_sb", [P, C])
        wr_sb = sb("wr_sb", [P, NE])
        bias_sb = sb("bias_sb", [P, NE])
        wgs_sb = sb("wgs_sb", [P, I])
        wds_sb = sb("wds_sb", [I, C])
        wc_sb = sb("wc_sb", [P, C])
        rpos = sb("rpos", [P, D])
        bdmg_sb = sb("bdmg_sb", [P, 1])
        hbout = sb("hbout", [P, 1])
        wsel = sb("wsel", [P, 2, 4, 32])
        tri = sb("tri", [P, P], BF16)
        ones = sb("ones", [P, P], BF16)
        carry = sb("carry", [P, NE])
        iota_e = sb("iota_e", [P, NE])
        tile_id = sb("tile_id", [P, 6])
        mhalf = sb("mhalf", [P, J])

        zero = sb("zero", [P, 2048])
        slots_zeroed = sem("slots_zeroed")

        with ExitStack() as c:
            mask_sb = sb("mask_sb", [P, D], F32, c)
            bm = sb("bm", [P, HH], F32, c)
            wdT = sb("wdT", [P, HG, C], F32, c)
            bd = sb("bd", [P, 2, P], F32, c)
            wst = sb("wst", [P, 2, E], F32, c)
            wcol = sb("wcol", [P, 2], F32, c)
            wpos_sb = sb("wpos_sb", [E, P], F32, c)
            rel_sb = sb("rel_sb", [E, D], F32, c)
            bout_sb = sb("bout_sb", [P, 1], F32, c)
            psw = c.enter_context(nc.psum_tensor("psw", [P, 5, 512], F32))
            loaded = sem("const_loaded")
            zeroed = sem("const_zeroed")
            filled = sem("const_filled")
            pool_step = sem("const_pool_step")
            blockmask_ready = sem("blockmask_ready")
            bd_ready = sem("bd_ready")
            w1_done = sem("w1_done")
            with nc.Block() as block:
                @block.sync
                def _(sp):
                    for dst, src in ((wdT[:], w_dispT.rearrange("(g p) c -> p g c", p=P)), (wval_sb[:], w_val),
                                     (wst[:, 0, :], w_strain), (wst[:, 1, :], w_dmg), (wcol[:, 0:1], w_bond),
                                     (wcol[:, 1:2], w_dmg_out), (wpos_sb[:], w_pos), (rel_sb[:], relT),
                                     (bout_sb[:], b_dmg_out), (bdmg_sb[:], b_dmg), (wr_sb[:], router_wT),
                                     (wgs_sb[:], w_gate_sharedT), (wds_sb[:], w_down_sharedT),
                                     (wc_sb[:], w_cproj), (bias_sb[:], expert_bias.partition_broadcast(P))):
                        sp.dma_start(dst, src).then_inc(loaded, 16)
                    sp.wait_ge(zeroed, 1)
                    sp.dma_start(band_dram.rearrange("s j p f -> p (s j) f"),
                                 zero[:, 0:BANDW].unsqueeze(1).to_broadcast([P, 2 * J, BANDW])).then_inc(filled, 16)
                    for i in range(2 * HG):
                        sp.dma_start(s_dram[i, :, :, 0:PAD].rearrange("b p t -> p b t"),
                                     zero[:, 0:B * PAD].rearrange("p (b t) -> p b t", b=B)).then_inc(filled, 16)
                    for lo in (0, PAD + T):
                        sp.dma_start(val_dram[:, lo:lo + PAD, :].rearrange("b p c -> p b c"),
                                     zero[0:PAD, 0:B * C].rearrange("p (b c) -> p b c", b=B)).then_inc(filled, 16)
                    sp.dma_start(mask_dram[1:CB].rearrange("n p d -> p n d"),
                                 zero[:, 0:(CB - 1) * D].rearrange("p (n d) -> p n d", n=CB - 1)).then_inc(filled, 16)
                    sp.wait_ge(pool_step, 6)
                    sp.dma_start(mask_dram[0], mask_sb[:]).then_inc(filled, 16)
                    sp.wait_ge(filled, 16 * (1 + 2 * HG + 2 + 2))
                    nfill = NSLOT * C // P // 2048
                    sp.dma_start(xslot_dram.rearrange("(p r) c -> p (r c)", p=P).rearrange("p (n f) -> p n f", n=nfill),
                                 zero[:].unsqueeze(1).to_broadcast([P, nfill, 2048])).then_inc(slots_zeroed, 16)

                @block.gpsimd
                def _(pool):
                    pool.memset(bm[:], 1.0).then_inc(pool_step, 1)
                    pool.wait_ge(pool_step, 1)
                    pool.affine_select(out=bm[:], in_=bm[:], compare_op=ALU.is_ge, fill=0.0, base=0,
                                       pattern=[[-E, HH]], channel_multiplier=1).then_inc(pool_step, 1)
                    pool.wait_ge(pool_step, 2)
                    pool.affine_select(out=bm[:], in_=bm[:], compare_op=ALU.is_ge, fill=0.0, base=E - 1,
                                       pattern=[[E, HH]], channel_multiplier=-1).then_inc(blockmask_ready, 1)
                    pool.memset(ident[:], 0.0).then_inc(pool_step, 1)
                    pool.memset(mask_sb[:], 0.0).then_inc(pool_step, 1)
                    pool.memset(tri[:], 1.0)
                    pool.memset(ones[:], 1.0)
                    pool.memset(mhalf[:], -0.5).then_inc(pool_step, 1)
                    pool.wait_ge(pool_step, 5)
                    pool.affine_select(out=mask_sb[:], in_=mask_sb[:], compare_op=ALU.is_ge, fill=NEG,
                                       base=-(D - 1), pattern=[[1, D]], channel_multiplier=1).then_inc(pool_step, 1)
                    pool.affine_select(out=ident[:], in_=ident[:], compare_op=ALU.not_equal, fill=1.0, base=0,
                                       pattern=[[-1, P]], channel_multiplier=1)
                    pool.affine_select(out=tri[:], in_=tri[:], compare_op=ALU.is_gt, fill=0.0, base=0,
                                       pattern=[[1, P]], channel_multiplier=-1)
                    pool.iota(iota_e[:], pattern=[[1, NE]], base=0, channel_multiplier=0,
                              allow_small_or_imprecise_dtypes=True)
                    pool.iota(tile_id[:], pattern=[[P, 6]], base=0, channel_multiplier=1,
                              allow_small_or_imprecise_dtypes=True).then_inc(pool_step, 1)

                @block.vector
                def _(dve):
                    dve.memset(zero[:], 0.0).then_inc(zeroed, 1)
                    dve.memset(wsel[:], 0.0).then_inc(zeroed, 1)
                    dve.memset(carry[:], 0.0)
                    dve.wait_ge(loaded, 16 * 15)
                    dve.wait_ge(blockmask_ready, 1)
                    dve.wait_ge(zeroed, 2)
                    for ty in range(2):
                        for h in range(HH):
                            last = dve.tensor_scalar(bd[:, ty, h * E:(h + 1) * E], wst[:, ty, :], bm[:, h:h + 1],
                                                     None, ALU.mult)
                        last.then_inc(bd_ready, 1)
                        for q in range(4):
                            dve.tensor_scalar(wsel[:, ty, q, HH * q:HH * (q + 1)], bm[:], wcol[:, ty:ty + 1],
                                              None, ALU.mult)
                    dve.tensor_scalar(hbout[:], bout_sb[:], 0.5, None, ALU.mult)
                    dve.wait_ge(w1_done, 1)
                    for i in range(2 * HG):
                        dve.tensor_copy(w1[:, i, :], psw[:, i, 0:P])
                    dve.tensor_copy(rpos[:], psw[:, 4, 0:D])

                @block.tensor
                def _(pe):
                    pe.wait_ge(loaded, 16 * 15)
                    for ty in range(2):
                        pe.wait_ge(bd_ready, ty + 1)
                        for g in range(HG):
                            pe.matmul(psw[:, ty * HG + g, 0:P], wdT[:, g, :], bd[:, ty, :], start=True, stop=True)
                    pe.matmul(psw[:, 4, 0:D], wpos_sb[:], rel_sb[:], start=True, stop=True).then_inc(w1_done, 1)

        with ExitStack() as c:
            xin = sb("xin", [P, 2, J, C], F32, c)
            xn = sb("xn", [P, J, C], F32, c)
            xT = sb("xT", [P, TC], F32, c)
            st6 = sb("st6", [P, J, 6], F32, c)
            mv = sb("mv", [P, J, 2], F32, c)
            ve = sb("ve", [P, J], F32, c)
            rstd = sb("rstd", [P, J], F32, c)
            s_sb = sb("s_sb", [P, 2 * HG, TC], F32, c)
            v_sb = sb("v_sb", [P, J, C], F32, c)
            probs = sb("probs", [P, J, NE], F32, c)
            sig_h = sb("sig_h", [I, TC], F32, c)
            act_h = sb("act_h", [I, TC], F32, c)
            part_sb = sb("part_sb", [P, J, C], F32, c)
            top = sb("top", [P, J, TOPK], F32, c)
            topi = sb("topi", [P, J, TOPK], U32, c)
            left = sb("left", [P, J, NE], F32, c)
            chosen = sb("chosen", [P, J, NE], BF16, c)
            gsum = sb("gsum", [P, J], F32, c)
            ginv = sb("ginv", [P, J], F32, c)
            rank_sb = sb("rank_sb", [P, J, NE], F32, c)
            ps_t = c.enter_context(nc.psum_tensor("ps_t", [P, TC], F32))
            ps_s = c.enter_context(nc.psum_tensor("ps_s", [P, 2, TC], F32))
            ps_v = c.enter_context(nc.psum_tensor("ps_v", [P, J, C], F32))
            ps_r = c.enter_context(nc.psum_tensor("ps_r", [P, 2, 512], F32))
            ps_h = c.enter_context(nc.psum_tensor("ps_h", [P, TC], F32))
            ps_y = c.enter_context(nc.psum_tensor("ps_y", [P, J, C], F32))
            x_loaded = [sem(f"x_loaded{u}") for u in range(2)]
            x_free = [sem(f"x_free{u}") for u in range(2)]
            var_ready, rstd_ready, xn_ready = sem("var_ready"), sem("rstd_ready"), sem("xn_ready")
            stats_ready = sem("stats_ready")
            xt_done, xt_copied = sem("xt_done"), sem("xt_copied")
            s_done, s_evac_act, s_evac_dve = sem("s_done"), sem("s_evac_act"), sem("s_evac_dve")
            v_done, v_evac = sem("v_done"), sem("v_evac")
            r_done, logits_ready, probs_ready = sem("r_done"), sem("logits_ready"), sem("probs_ready")
            h_done, sig_ready, acth_ready, y_done = sem("h_done"), sem("sig_ready"), sem("acth_ready"), sem("y_done")
            part_ready, top_step, chosen_ready = sem("part_ready"), sem("top_step"), sem("chosen_ready")
            rank_done, rank_ready, carry_used = sem("rank_done"), sem("rank_ready"), sem("carry_used")
            stored = {n: sem(f"stored_{n}") for n in ("xn", "s", "v", "part", "rank")}

            def rank_ps(j):
                return ps_r[:, j // 2, (j % 2) * NE:(j % 2 + 1) * NE]

            with nc.Block() as block:
                @block.sync
                def _(sp):
                    def body(k):
                        for u in range(2):
                            it = k * 2 + u
                            if some(k):
                                sp.wait_ge(x_free[u], k)
                            sp.dma_start(xin[:, u], chunk_rows(x_rows, it)).then_inc(x_loaded[u], 16)
                            sp.wait_ge(xn_ready, J * it + J)
                            sp.dma_start(chunk_rows(xn_dram, it), xn[:]).then_inc(stored["xn"], 16)
                            sp.wait_ge(part_ready, it + 1)
                            sp.dma_start(chunk_rows(part_dram, it), part_sb[:]).then_inc(stored["part"], 16)
                    peeled(sp, NCH // 2, body)
                    for s in stored.values():
                        sp.wait_ge(s, 16 * NCH)

                @block.gpsimd
                def _(pool):
                    def chunk(b, tc, it):
                        pool.wait_ge(var_ready, it + 1)
                        pool.tensor_tensor(rstd[:], ve[:], mhalf[:], ALU.pow).then_inc(rstd_ready, 1)
                        pool.wait_ge(s_evac_act, 2 * it + 2)
                        pool.wait_ge(s_evac_dve, 2 * it + 2)
                        pool.dma_start(s_dram[:, bass.ds(b, 1), :, bass.ds(tc * TC + PAD, TC)]
                                       .rearrange("i b p t -> p (i b) t"), s_sb[:]).then_inc(stored["s"], 16)
                        pool.wait_ge(v_evac, it + 1)
                        pool.dma_start(val_dram[bass.ds(b, 1), bass.ds(tc * TC + PAD, TC), :]
                                       .rearrange("b (j p) c -> p (b j) c", p=P), v_sb[:]).then_inc(stored["v"], 16)
                        pool.wait_ge(rank_ready, it + 1)
                        pool.dma_start(chunk_rows(rank_dram, it), rank_sb[:]).then_inc(stored["rank"], 16)

                    for tc in range(CB):
                        chunk(0, tc, tc)
                    with pool.Fori(1, B) as b:
                        with pool.Fori(0, CB) as tc:
                            chunk(b, tc, b * CB + tc)

                @block.scalar
                def _(act):
                    def body(it):
                        act.wait_ge(xt_done, it + 1)
                        act.activation(xT[:], ps_t[:], ACT.Copy).then_inc(xt_copied, 1)
                        if some(16 * it):
                            act.wait_ge(stored["s"], 16 * it)
                        for i in (0, 2):
                            act.wait_ge(s_done, 4 * it + i + 1)
                            act.activation(s_sb[:, i, :], ps_s[:, 0, :], ACT.Copy).then_inc(s_evac_act, 1)
                        act.wait_ge(logits_ready, it + 1)
                        act.activation(probs[:], probs[:], ACT.Sigmoid).then_inc(probs_ready, 1)
                        act.wait_ge(h_done, it + 1)
                        act.activation(sig_h[:], ps_h[0:I, :], ACT.Sigmoid).then_inc(sig_ready, 1)
                    peeled(act, NCH, body)
                @block.tensor
                def _(pe):
                    def body(it):
                        if some(it):
                            pe.wait_ge(rank_ready, it)
                        for j in range(J):
                            pe.wait_ge(xn_ready, J * it + j + 1)
                            last = pe.transpose(ps_t[:, j * P:(j + 1) * P], xn[:, j, :], ident[:])
                        last.then_inc(xt_done, 1)
                        pe.wait_ge(xt_copied, it + 1)
                        for j in range(J):
                            last = pe.matmul(rank_ps(j), xT[:, j * P:(j + 1) * P], wr_sb[:], start=True, stop=True)
                        last.then_inc(r_done, 1)
                        if some(it):
                            pe.wait_ge(acth_ready, it)
                        pe.matmul(ps_h[0:I, :], wgs_sb[:], xT[:], start=True, stop=True).then_inc(h_done, 1)
                        for i in range(4):
                            if some(2 * it + i // 2):
                                pe.wait_ge((s_evac_act, s_evac_dve)[i % 2], 2 * it + i // 2)
                            pe.matmul(ps_s[:, i % 2, :], w1[:, i, :], xT[:], start=True, stop=True).then_inc(s_done, 1)
                        if some(it):
                            pe.wait_ge(v_evac, it)
                        for j in range(J):
                            last = pe.matmul(ps_v[:, j, :], xT[:, j * P:(j + 1) * P], wval_sb[:], start=True, stop=True)
                        last.then_inc(v_done, 1)
                        pe.wait_ge(acth_ready, it + 1)
                        if some(it):
                            pe.wait_ge(part_ready, it)
                        for j in range(J):
                            last = pe.matmul(ps_y[:, j, :], act_h[:, j * P:(j + 1) * P], wds_sb[:], start=True, stop=True)
                        last.then_inc(y_done, 1)
                        pe.wait_ge(chosen_ready, it + 1)
                        for j in range(J):
                            for i in range(j + 1):
                                pe.matmul(rank_ps(j), tri[:] if i == j else ones[:], chosen[:, i, :],
                                          start=(i == 0), stop=(i == j))
                        for j in range(J):
                            last = pe.matmul(ps_t[:, 0:NE], ones[:], chosen[:, j, :], start=(j == 0), stop=(j == J - 1))
                        last.then_inc(rank_done, 1)
                    peeled(pe, NCH, body)
                @block.vector
                def _(dve):
                    def body(k):
                        for u in range(2):
                            it = k * 2 + u
                            dve.wait_ge(x_loaded[u], 16 * k + 16)
                            for j in range(J):
                                dve.bn_stats(st6[:, j, :], xin[:, u, j, :]).then_inc(stats_ready, 1)
                            dve.wait_ge(stats_ready, 2 * J * it + J)
                            dve.sem_inc(held, 1)
                            for j in range(J):
                                dve.bn_aggr(mv[:, j, :], st6[:, j, :]).then_inc(stats_ready, 1)
                            dve.wait_ge(stats_ready, 2 * J * it + 2 * J)
                            dve.tensor_scalar(ve[:], mv[:, :, 1], LN_EPS, None, ALU.add).then_inc(var_ready, 1)
                            dve.wait_ge(rstd_ready, it + 1)
                            if some(16 * it):
                                dve.wait_ge(stored["xn"], 16 * it)
                            for j in range(J):
                                dve.tensor_scalar(xn[:, j, :], xin[:, u, j, :], mv[:, j, 0:1], rstd[:, j:j + 1],
                                                  ALU.subtract, ALU.mult).then_inc(xn_ready, 1)
                            dve.wait_ge(r_done, it + 1)
                            dve.tensor_tensor(probs[:].rearrange("p (a b) e -> p a b e", a=2),
                                              ps_r[:, :, 0:2 * NE].rearrange("p a (b e) -> p a b e", b=2),
                                              bias_sb[:].unsqueeze(1).unsqueeze(1).to_broadcast([P, 2, 2, NE]),
                                              ALU.add).then_inc(logits_ready, 1)
                            if some(16 * it):
                                dve.wait_ge(stored["s"], 16 * it)
                            for i in (1, 3):
                                dve.wait_ge(s_done, 4 * it + i + 1)
                                dve.tensor_copy(s_sb[:, i, :], ps_s[:, 1, :]).then_inc(s_evac_dve, 1)
                            dve.wait_ge(sig_ready, it + 1)
                            dve.tensor_tensor(act_h[:], sig_h[:], ps_h[0:I, :], ALU.mult).then_inc(acth_ready, 1)
                            dve.wait_ge(v_done, it + 1)
                            if some(16 * it):
                                dve.wait_ge(stored["v"], 16 * it)
                            dve.tensor_copy(v_sb[:], ps_v[:]).then_inc(v_evac, 1)
                            dve.wait_ge(probs_ready, it + 1)
                            dve.sem_inc(held, 1)
                            for j in range(J):
                                dve.max(top[:, j, :], probs[:, j, :]).then_inc(top_step, 1)
                            dve.wait_ge(top_step, 4 * J * it + J)
                            dve.sem_inc(held, 1)
                            for j in range(J):
                                dve.max_index(topi[:, j, :], top[:, j, :], probs[:, j, :]).then_inc(top_step, 1)
                            for j in range(J):
                                dve.match_replace(left[:, j, :], top[:, j, :], probs[:, j, :], -1.0).then_inc(top_step, 1)
                            if some(4 * J * it + 3 * J):
                                dve.wait_ge(top_step, 4 * J * it + 3 * J)
                            dve.tensor_scalar(chosen[:], left[:], 0.0, None, ALU.is_lt).then_inc(chosen_ready, 1)
                            dve.tensor_reduce(gsum[:], top[:], AX.X, ALU.add).then_inc(top_step, 1)
                            dve.wait_ge(top_step, 4 * J * it + 3 * J + 1)
                            dve.tensor_scalar(gsum[:], gsum[:], GATE_EPS, None, ALU.add).then_inc(top_step, 1)
                            dve.wait_ge(top_step, 4 * J * it + 3 * J + 2)
                            dve.reciprocal(ginv[:], gsum[:]).then_inc(top_step, 1)
                            dve.tensor_copy(expert_all[:, bass.ds(it * J * TOPK, J * TOPK)],
                                            topi[:].rearrange("p j k -> p (j k)"))
                            dve.wait_ge(top_step, 4 * J * it + 3 * J + 3)
                            dve.tensor_tensor(top[:], top[:], ginv[:].unsqueeze(2).to_broadcast([P, J, TOPK]),
                                              ALU.mult).then_inc(top_step, 1)
                            dve.wait_ge(top_step, 4 * J * it + 3 * J + 4)
                            dve.tensor_scalar(gates_all[:, bass.ds(it * J * TOPK, J * TOPK)],
                                              top[:].rearrange("p j k -> p (j k)"), ROUTED_SCALE, None, ALU.mult)
                            dve.wait_ge(y_done, it + 1)
                            if some(16 * it):
                                dve.wait_ge(stored["part"], 16 * it)
                            dve.tensor_tensor(part_sb[:], ps_y[:], xin[:, u], ALU.add).then_inc(part_ready, 1)
                            dve.wait_ge(part_ready, it + 1)
                            dve.sem_inc(x_free[u], 1)
                            dve.wait_ge(rank_done, it + 1)
                            if some(16 * it):
                                dve.wait_ge(stored["rank"], 16 * it)
                            dve.tensor_tensor(rank_sb[:].rearrange("p (a b) e -> p a b e", a=2),
                                              ps_r[:, :, 0:2 * NE].rearrange("p a (b e) -> p a b e", b=2),
                                              carry[:].unsqueeze(1).unsqueeze(1).to_broadcast([P, 2, 2, NE]), ALU.add)\
                                .then_inc(carry_used, 1)
                            dve.wait_ge(carry_used, it + 1)
                            dve.tensor_tensor(carry[:], carry[:], ps_t[:, 0:NE], ALU.add).then_inc(rank_ready, 1)
                            dve.wait_ge(rank_ready, it + 1)
                    peeled(dve, NCH // 2, body)
        with ExitStack() as c:
            ci = sb("ci", [P, NE], I32, c)
            ntl = sb("ntl", [P, NE], F32, c)
            cum = [sb(f"cum{i}", [P, NE], F32, c) for i in range(2)]
            le = sb("le", [P, 6, NE], F32, c)
            tef = sb("tef", [P, 6], F32, c)
            tei = sb("tei", [P, 6], I32, c)
            place_step, tiles_known = sem("place_step"), sem("tiles_known")
            te_stored = sem("te_stored")
            with nc.Block() as block:
                @block.vector
                def _(dve):
                    n = 0

                    def then(ins):
                        nonlocal n
                        n += 1
                        ins.then_inc(place_step, 1)
                        if some(n):
                            dve.wait_ge(place_step, n)

                    then(dve.tensor_scalar(ci[:], carry[:], float(P - 1), None, ALU.add))
                    then(dve.tensor_scalar(ci[:], ci[:], 7, None, ALU.logical_shift_right))
                    then(dve.tensor_copy(ntl[:], ci[:]))
                    src, s = ntl, 1
                    i = 0
                    while s < NE:
                        dst = cum[i % 2]
                        dve.tensor_copy(dst[:, 0:s], src[:, 0:s])
                        then(dve.tensor_tensor(dst[:, s:NE], src[:, s:NE], src[:, 0:NE - s], ALU.add))
                        src, s, i = dst, 2 * s, i + 1
                    for g in range(6):
                        last = dve.tensor_scalar(le[:, g, :], src[:], tile_id[:, g:g + 1], None, ALU.is_le)
                    then(last)
                    then(dve.tensor_reduce(tef[:], le[:], AX.X, ALU.add))
                    then(dve.tensor_scalar(tei[:], tef[:], float(NE - 1), None, ALU.min))
                    dve.sem_inc(tiles_known, 1)
                    then(dve.tensor_tensor(carry[:], src[:], ntl[:], ALU.subtract))
                    then(dve.tensor_scalar(carry[:], carry[:], float(P), None, ALU.mult))

                @block.sync
                def _(sp):
                    sp.wait_ge(tiles_known, 1)
                    sp.dma_start(tile_expert_dram.rearrange("o (g p) -> p (o g)", p=P), tei[:], allow_slow_non_contiguous=True)\
                        .then_inc(te_stored, 16)
                    sp.wait_ge(te_stored, 16)

        with ExitStack() as c:
            xr = sb("xr", [P, J, C], F32, c)
            rk = sb("rk", [P, J, NE], F32, c)
            ex = sb("ex", [P, J * TOPK], F32, c)
            pick = sb("pick", [P, J * TOPK, NE], F32, c)
            slotf = sb("slotf", [P, J * TOPK], F32, c)
            sloti = sb("sloti", [P, J * TOPK], U32, c)
            rows_in, ranks_in = sem("rows_in"), sem("ranks_in")
            slot_step, slots_ready, scattered = sem("slot_step"), sem("slots_ready"), sem("scattered")
            NS = J * TOPK
            with nc.Block() as block:
                @block.sync
                def _(sp):
                    def body(it):
                        if some(it):
                            sp.wait_ge(slots_ready, it)
                        sp.dma_start(rk[:], chunk_rows(rank_dram, it)).then_inc(ranks_in, 16)
                        if some(16 * NS * it):
                            sp.wait_ge(scattered, 16 * NS * it)
                        sp.dma_start(xr[:], chunk_rows(xn_dram, it)).then_inc(rows_in, 16)
                    peeled(sp, NCH, body)
                @block.vector
                def _(dve):
                    def body(it):
                        dve.wait_ge(ranks_in, 16 * it + 16)
                        dve.tensor_tensor(rk[:], rk[:], carry[:].unsqueeze(1).to_broadcast([P, J, NE]),
                                          ALU.add).then_inc(slot_step, 1)
                        dve.tensor_copy(ex[:], expert_all[:, bass.ds(it * NS, NS)]).then_inc(slot_step, 1)
                        dve.wait_ge(slot_step, (2 + NS) * it + 2)
                        for n in range(NS):
                            dve.scalar_tensor_tensor(out=pick[:, n, :], in0=iota_e[:], scalar=ex[:, n:n + 1],
                                                     in1=rk[:, n // TOPK, :], op0=ALU.is_equal, op1=ALU.mult,
                                                     accum_out=slotf[:, n:n + 1]).then_inc(slot_step, 1)
                        dve.wait_ge(slot_step, (2 + NS) * it + 2 + NS)
                        if some(16 * NS * it):
                            dve.wait_ge(scattered, 16 * NS * it)
                        dve.tensor_copy(slots_all[:, bass.ds(it * NS, NS)], slotf[:])
                        dve.tensor_copy(sloti[:], slotf[:]).then_inc(slots_ready, 1)
                    peeled(dve, NCH, body)
                @block.gpsimd
                def _(pool):
                    def body(it):
                        pool.wait_ge(rows_in, 16 * it + 16)
                        pool.wait_ge(slots_ready, it + 1)
                        pool.sem_inc(held, 1)
                        for n in range(NS):
                            pool.indirect_dma_start(xslot_dram, bass.IndirectOffsetOnAxis(ap=sloti[:, n:n + 1], axis=0),
                                                    xr[:, n // TOPK, :], None).then_inc(scattered, 16)
                    pool.wait_ge(slots_zeroed, 16)
                    peeled(pool, NCH, body)
                    pool.wait_ge(scattered, 16 * NS * NCH)

        with ExitStack() as c:
            NI = 16
            CH = 4
            u_dve = sb("u_dve", [P, 3, 8, TC], F32, c)
            u_pool = sb("u_pool", [P, 2, 8, TC], F32, c)
            s_win = sb("s_win", [P, HG, 2, SW], F32, c)
            tanh_sb = sb("tanh_sb", [P, 2, TC], F32, c)
            lg = sb("lg", [P, 2, CH, TC], F32, c)
            ml = sb("ml", [P, J, D, HH], F32, c)
            mx = sb("mx", [P, J, HH], F32, c)
            wsum = sb("wsum", [P, J, HH], F32, c)
            winv = sb("winv", [P, J, HH], F32, c)
            band = sb("band", [P, J, BANDW], F32, c)
            at_sb = sb("at_sb", [P, 2, 4, P], F32, c)
            v_raw = sb("v_raw", [P, 2 * J, C], F32, c)
            v_msk = sb("v_msk", [P, 2 * J, H * 32], F32, c)
            mask_t = sb("mask_t", [P, D], F32, c)
            oT_sb = sb("oT_sb", [P, TC], F32, c)
            part_t = sb("part_t", [P, J, C], F32, c)
            y_sb = sb("y_sb", [P, J, C], F32, c)
            ps_l = c.enter_context(nc.psum_tensor("ps_l", [P, 2, 2, TC], F32))
            ps_o = c.enter_context(nc.psum_tensor("ps_o", [P, TC], F32))
            ps_u = c.enter_context(nc.psum_tensor("ps_u", [P, TC], F32))
            win_loaded = [sem(f"win_loaded{g}") for g in range(HG)]
            sub_dve, sub_pool, gelu_done, item_done = sem("sub_dve"), sem("sub_pool"), sem("gelu_done"), sem("item_done")
            tanh_done, logits_in = sem("tanh_done"), sem("logits_in")
            turned, tokens_in, max_in, centred, exped = sem("turned"), sem("tokens_in"), sem("max_in"), sem("centred"), sem("exped")
            masked, sum_in, inv_in, normed = sem("masked"), sem("sum_in"), sem("inv_in"), sem("normed")
            band_out, band_in, band_turned, band_copied = sem("band_out"), sem("band_in"), sem("band_turned"), sem("band_copied")
            av_done, v_loaded, v_spread = sem("av_done"), sem("v_loaded"), sem("v_spread")
            mask_loaded, part_loaded = sem("mask_loaded"), sem("part_loaded")
            o_copied, cproj_done, y_copied = sem("o_copied"), sem("cproj_done"), sem("y_copied")
            y_ready, y_stored = sem("y_ready"), sem("y_stored")
            v_zeroed = sem("v_zeroed")
            NSTEP = 2 * NCH
            on_pool = POOL_ITEMS
            NP = len(on_pool)
            dve_of = [sum(q % 4 not in on_pool for q in range(n + 1)) for n in range(NI)]
            pool_of = [n + 1 - dve_of[n] for n in range(NI)]
            ND, NPI = dve_of[-1], pool_of[-1]

            def steps(e, step):
                for s, st in enumerate(("i", "is", "isa", "isat")):
                    step(s, s // 2, s % 2, st)
                with e.Fori(2, NCH) as it:
                    for par in range(2):
                        step(it * 2 + par, it, par, "isat")
                for s, st in enumerate(("sat", "at", "t"), NSTEP):
                    step(s, s // 2, s % 2, st)

            def offsets(n):
                return n // 4, 16 * (n // 4) + 8 * (n % 4 // 2), n % 2

            def windows(par, ty, d0, nd):
                row = s_win[:, par, ty, d0 + 1:d0 + 1 + TC]
                return bass.AP(row.tensor, row.offset, [list(row.ap[0]), [1, nd], [1, TC]])

            def item_buffer(n):
                if n % 4 in on_pool:
                    return u_pool[:, (pool_of[n] - 1) % 2]
                return u_dve[:, (n % 4 - sum(q < n % 4 for q in on_pool))]

            def buffer_free(n):
                if n % 4 in on_pool:
                    return n + 1 - 8 // NP
                return n - 3

            with nc.Block() as block:
                @block.sync
                def _(sp):
                    def load_windows(b, tc, it, par):
                        if not isinstance(it, int) or it > 0:
                            if some(ND * (2 * it + par - 1)):
                                sp.wait_ge(sub_dve, ND * (2 * it + par - 1))
                                sp.sem_inc(held, 1)
                            if some(NPI * (2 * it + par - 1)):
                                sp.wait_ge(sub_pool, NPI * (2 * it + par - 1))
                                sp.sem_inc(held, 1)
                        for ty in range(2):
                            sp.dma_start(s_win[:, par, ty, :],
                                         s_dram[ty * HG + par, bass.ds(b, 1), :, bass.ds(tc * TC, SW)]
                                         .rearrange("b p t -> p (b t)")).then_inc(win_loaded[par], 16)

                    def load_chunk(b, tc, it):
                        if some(2 * it):
                            sp.wait_ge(masked, 2 * it)
                        sp.dma_start(mask_t[:], mask_dram[bass.ds(tc, 1)].rearrange("n p d -> p (n d)"))\
                            .then_inc(mask_loaded, 16)
                        if some(it):
                            sp.wait_ge(v_spread, it)
                        for w in range(2 * J):
                            sp.dma_start(v_raw[:, w, :],
                                         val_dram[bass.ds(b, 1), bass.ds(tc * TC + w * HALF + 1, P), :]
                                         .rearrange("b p c -> p (b c)")).then_inc(v_loaded, 16)

                    def band_trip(u):
                        sp.wait_ge(normed, u + 1)
                        sp.sem_inc(held, 1)
                        if some(16 * u):
                            sp.wait_ge(band_in, 16 * u)
                            sp.sem_inc(held, 1)
                        for h in range(2):
                            first = band_dram[0, :, h * HALF:(h + 1) * HALF, :]
                            skewed = bass.AP(first.tensor, first.offset,
                                             [[BANDW + HH, HALF], [P * BANDW, J], [1, D * HH]])
                            sp.dma_start(skewed, ml[h * HALF:(h + 1) * HALF].rearrange("p j d h -> p j (d h)"))\
                                .then_inc(band_out, 16)
                        sp.wait_ge(band_out, 32 * u + 32)
                        sp.sem_inc(held, 1)
                        if some(8 * u):
                            sp.wait_ge(band_turned, 8 * u)
                        sp.dma_start(band[:], band_dram[0].rearrange("j p f -> p j f")).then_inc(band_in, 16)

                    def load_part(it):
                        if some(16 * it):
                            sp.wait_ge(y_stored, 16 * it)
                        sp.dma_start(part_t[:], chunk_rows(part_dram, it)).then_inc(part_loaded, 16)

                    def store_y(it):
                        sp.wait_ge(y_ready, it + 1)
                        sp.dma_start(chunk_rows(attn_dram, it), y_sb[:]).then_inc(y_stored, 16)

                    def chunk(b, tc, it):
                        full = not isinstance(it, int) or it > 1
                        load_windows(b, tc, it, 0)
                        if full or it > 0:
                            band_trip(2 * it - 2)
                        load_windows(b, tc, it, 1)
                        if full:
                            load_part(it - 2)
                            store_y(it - 2)
                        load_chunk(b, tc, it)
                        if full or it > 0:
                            band_trip(2 * it - 1)

                    for tc in range(CB):
                        chunk(0, tc, tc)
                    with sp.Fori(1, B) as b:
                        with sp.Fori(0, CB) as tc:
                            chunk(b, tc, b * CB + tc)
                    band_trip(NSTEP - 2)
                    load_part(NCH - 2)
                    store_y(NCH - 2)
                    band_trip(NSTEP - 1)
                    load_part(NCH - 1)
                    store_y(NCH - 1)
                    sp.wait_ge(y_stored, 16 * NCH)

                @block.gpsimd
                def _(pool):
                    pool.memset(v_msk[:], 0.0).then_inc(v_zeroed, 1)
                    pool.wait_ge(v_zeroed, 1)

                    def spread(it):
                        pool.wait_ge(v_loaded, 16 * 2 * J * (it + 1))
                        if some(16 * it):
                            pool.wait_ge(av_done, 16 * it)
                            pool.sem_inc(held, 1)
                        for w in range(2 * J):
                            dst = v_msk[:, w, 0:HS]
                            last = pool.tensor_copy(
                                bass.AP(dst.tensor, dst.offset, [list(dst.ap[0]), [4 * 32, H // 4], [32 + HS, 4], [1, HS]]),
                                v_raw[:, w, :].rearrange("p (g i e) -> p g i e", g=H // 4, i=4))
                        last.then_inc(v_spread, 1)

                    def step(s, it, par, st):
                        for n in range(NI):
                            cgrp, d0, ty = offsets(n)
                            if "i" in st and n % 4 in on_pool:
                                if pool_of[n] == 1:
                                    pool.wait_ge(win_loaded[par], 32 * it + 32)
                                if some(NI * s + buffer_free(n)):
                                    pool.wait_ge(item_done, NI * s + buffer_free(n))
                                pool.tensor_tensor(
                                    item_buffer(n), windows(par, ty, d0, 8),
                                    s_win[:, par, ty, PAD:PAD + TC].unsqueeze(1).to_broadcast([P, 8, TC]),
                                    ALU.subtract).then_inc(sub_pool, 1)
                            if "a" in st and n == 3 and par == 0:
                                spread(it - 1)
                            if "t" in st and n == 5 and par == 0:
                                if some(it - 1):
                                    pool.wait_ge(y_copied, it - 1)
                                if some(16 * (it - 1)):
                                    pool.wait_ge(part_loaded, 16 * (it - 1))
                                pool.tensor_tensor(y_sb[:], y_sb[:], part_t[:], ALU.add).then_inc(y_ready, 1)
                            if "s" in st and n == 15:
                                pool.wait_ge(inv_in, s)
                                pool.tensor_tensor(ml[:], ml[:], winv[:].unsqueeze(2).to_broadcast([P, J, D, HH]),
                                                   ALU.mult).then_inc(normed, 1)

                    steps(pool, step)

                @block.scalar
                def _(act):
                    def step(s, it, par, st):
                        for n in range(NI):
                            cgrp, d0, ty = offsets(n)
                            if "i" in st:
                                if n % 4 in on_pool:
                                    if some(NPI * s + pool_of[n]):
                                        act.wait_ge(sub_pool, NPI * s + pool_of[n])
                                else:
                                    if some(ND * s + dve_of[n]):
                                        act.wait_ge(sub_dve, ND * s + dve_of[n])
                                u = item_buffer(n)
                                if ty:
                                    act.activation(u, u, ACT.Gelu, bias=bdmg_sb[:]).then_inc(gelu_done, 1)
                                else:
                                    act.activation(u, u, ACT.Gelu).then_inc(gelu_done, 1)
                            if n % 4 == 1 and ("i" in st if n > 1 else "s" in st):
                                k = 4 * s + cgrp - 1
                                act.wait_ge(item_done, 4 * k + 4)
                                if some(k - 1):
                                    act.wait_ge(logits_in, k - 1)
                                act.activation(tanh_sb[:, (cgrp - 1) % 2], ps_l[:, (cgrp - 1) % 2, 1], ACT.Tanh,
                                               bias=hbout[:], scale=0.5).then_inc(tanh_done, 1)
                            if "s" in st and 5 <= n <= 8:
                                j = n - 5
                                act.wait_ge(turned, 4 * (s - 1) + j + 1)
                                if some(32 * (s - 1)):
                                    act.wait_ge(band_out, 32 * (s - 1))
                                act.activation(ml[:, j].rearrange("p d h -> p (d h)"), ps_u[:], ACT.Copy)\
                                    .then_inc(tokens_in, 1)
                            if "s" in st and n == 13:
                                if some(4 * s):
                                    act.wait_ge(centred, 4 * s)
                                act.activation(ml[:], ml[:], ACT.Exp).then_inc(exped, 1)
                            for k, u in ((n - 9, s - 2) if n >= 9 and "a" in st else (0, None),
                                         (7, s - 3) if n == 0 and "t" in st else (0, None)):
                                if u is not None:
                                    act.wait_ge(band_turned, 8 * u + k + 1)
                                    if some(8 * u + k - 1):
                                        act.wait_ge(av_done, 8 * u + k - 1)
                                    act.activation(at_sb[:, k % 2].rearrange("p i t -> p (i t)"), ps_u[:], ACT.Copy)\
                                        .then_inc(band_copied, 1)
                            if "t" in st and par == 0 and n == 2:
                                if some(8 * (s - 2)):
                                    act.wait_ge(av_done, 8 * (s - 2))
                                act.activation(oT_sb[:], ps_o[:], ACT.Copy).then_inc(o_copied, 1)
                            if "t" in st and par == 0 and n == 4:
                                if some(it - 1):
                                    act.wait_ge(cproj_done, it - 1)
                                if some(16 * (it - 2)):
                                    act.wait_ge(y_stored, 16 * (it - 2))
                                act.activation(y_sb[:].rearrange("p j c -> p (j c)"), ps_u[:], ACT.Copy)\
                                    .then_inc(y_copied, 1)

                    steps(act, step)

                @block.vector
                def _(dve):
                    def step(s, it, par, st):
                        for n in range(NI):
                            cgrp, d0, ty = offsets(n)
                            if "i" in st and n % 4 not in on_pool:
                                if dve_of[n] == 1:
                                    dve.wait_ge(win_loaded[par], 32 * it + 32)
                                if some(NI * s + buffer_free(n)):
                                    dve.wait_ge(item_done, NI * s + buffer_free(n))
                                here = s_win[:, par, ty, PAD:PAD + TC]
                                if ty:
                                    last = dve.tensor_tensor(item_buffer(n), windows(par, ty, d0, 8),
                                                             here.unsqueeze(1).to_broadcast([P, 8, TC]), ALU.subtract)
                                else:
                                    for d in range(8):
                                        last = dve.scalar_tensor_tensor(
                                            out=item_buffer(n)[:, d, :], in0=s_win[:, par, ty, d0 + d + 1:d0 + d + 1 + TC],
                                            scalar=rpos[:, d0 + d:d0 + d + 1], in1=here, op0=ALU.add, op1=ALU.subtract)
                                last.then_inc(sub_dve, 1)
                            if n % 4 == 0 and ("i" in st if n > 4 else "s" in st):
                                k = 4 * s + cgrp - 2
                                dve.wait_ge(tanh_done, k + 1)
                                if n > 4:
                                    if some(4 * (s - 1)):
                                        dve.wait_ge(turned, 4 * (s - 1))
                                dve.scalar_tensor_tensor(out=lg[:, par if n > 4 else 1 - par, (cgrp - 2) % 4, :],
                                                         in0=tanh_sb[:, (cgrp - 2) % 2], scalar=-5.0,
                                                         in1=ps_l[:, (cgrp - 2) % 2, 0], op0=ALU.mult,
                                                         op1=ALU.add).then_inc(logits_in, 1)
                            if "s" in st and 8 <= n <= 11:
                                j = n - 8
                                dve.wait_ge(tokens_in, 4 * (s - 1) + j + 1)
                                if j == 0:
                                    if some(16 * ((it if par else it - 1) + 1)):
                                        dve.wait_ge(mask_loaded, 16 * ((it if par else it - 1) + 1))
                                    dve.tensor_tensor(ml[:, 0], ml[:, 0],
                                                      mask_t[:].unsqueeze(2).to_broadcast([P, D, HH]), ALU.add)\
                                        .then_inc(masked, 1)
                                    dve.wait_ge(masked, s)
                                dve.tensor_reduce(mx[:, j, :], ml[:, j].rearrange("p d h -> p h d"), AX.X, ALU.max)\
                                    .then_inc(max_in, 1)
                                dve.wait_ge(max_in, 4 * (s - 1) + j + 1)
                                dve.tensor_tensor(ml[:, j], ml[:, j], mx[:, j, :].unsqueeze(1).to_broadcast([P, D, HH]),
                                                  ALU.subtract).then_inc(centred, 1)
                            if "s" in st and n == 15:
                                dve.wait_ge(exped, s)
                                dve.tensor_reduce(wsum[:], ml[:].rearrange("p j d h -> p j h d"), AX.X, ALU.add)\
                                    .then_inc(sum_in, 1)
                                dve.wait_ge(sum_in, s)
                                dve.reciprocal(winv[:], wsum[:]).then_inc(inv_in, 1)

                    steps(dve, step)

                @block.tensor
                def _(pe):
                    def values(u, k, itu, g0):
                        j, g = k // 2, g0 + k % 2
                        if k == 0:
                            pe.wait_ge(v_spread, itu + 1)
                            if g0 == 0:
                                if some(itu):
                                    pe.wait_ge(o_copied, itu)
                        pe.wait_ge(band_copied, 8 * u + k + 1)
                        for half in range(2):
                            for i in range(4):
                                h = 4 * g + i
                                last = pe.matmul(
                                    ps_o[32 * g:32 * g + 32, j * P + half * HALF:j * P + (half + 1) * HALF],
                                    v_msk[:, 2 * j + half, 32 * h:32 * h + 32],
                                    at_sb[:, k % 2, i, half * HALF:(half + 1) * HALF],
                                    start=(i == 0), stop=(i == 3))
                        last.then_inc(av_done, 1)

                    def step(s, it, par, st):
                        for n in range(NI):
                            cgrp, d0, ty = offsets(n)
                            if "i" in st:
                                if n % 4 < 2:
                                    if some(4 * s + cgrp - 1):
                                        pe.wait_ge(logits_in, 4 * s + cgrp - 1)
                                pe.wait_ge(gelu_done, NI * s + n + 1)
                                for d in range(8):
                                    q, g = (d0 + d) % 16 // 4, d % 4
                                    last = pe.matmul(ps_l[32 * g:32 * g + 32, cgrp % 2, ty, :], wsel[:, ty, q, :],
                                                     item_buffer(n)[:, d, :], start=(q == 0), stop=(q == 3))
                                last.then_inc(item_done, 1)
                            if "t" in st and n < 2:
                                values(s - 3, 6 + n, it - 1 if par else it - 2, 2 - 2 * par)
                            if "t" in st and par == 0 and n == 3:
                                if some(it - 1):
                                    pe.wait_ge(o_copied, it - 1)
                                if some(8 * (s - 2)):
                                    pe.wait_ge(band_copied, 8 * (s - 2))
                                for j in range(J):
                                    last = pe.matmul(ps_u[:, j * P:(j + 1) * P], oT_sb[:, j * P:(j + 1) * P], wc_sb[:],
                                                     start=True, stop=True)
                                last.then_inc(cproj_done, 1)
                            if "s" in st and 4 <= n <= 7:
                                j = n - 4
                                if j == 0:
                                    if some(4 * s):
                                        pe.wait_ge(logits_in, 4 * s)
                                    if "t" in st:
                                        if some(it - 1 if par == 0 else 0):
                                            pe.wait_ge(y_copied, it - 1 if par == 0 else 0)
                                        if some(8 * (s - 2)):
                                            pe.wait_ge(band_copied, 8 * (s - 2))
                                if some(4 * (s - 1) + j):
                                    pe.wait_ge(tokens_in, 4 * (s - 1) + j)
                                for g in range(CH):
                                    last = pe.transpose(
                                        ps_u[:, P * g:P * g + P].rearrange("p (q g h) -> p g q h", g=4, h=HH),
                                        lg[:, 1 - par, g, j * P:(j + 1) * P], ident[:])
                                last.then_inc(turned, 1)
                            if "a" in st and n >= 8:
                                k = n - 8
                                if k == 0:
                                    if some(16 * (s - 1)):
                                        pe.wait_ge(band_in, 16 * (s - 1))
                                    if some(4 * s if "s" in st else 0):
                                        pe.wait_ge(tokens_in, 4 * s if "s" in st else 0)
                                    if some(it - 1 if "t" in st and par == 0 else 0):
                                        pe.wait_ge(y_copied, it - 1 if "t" in st and par == 0 else 0)
                                if some(8 * (s - 2) + k):
                                    pe.wait_ge(band_copied, 8 * (s - 2) + k)
                                for i in range(4):
                                    last = pe.transpose(ps_u[:, i * P:(i + 1) * P],
                                                        band[:, k // 2, 4 * (k % 2) + i:BANDW:HH], ident[:])
                                last.then_inc(band_turned, 1)
                                if k >= 2:
                                    values(s - 2, k - 2, it - 1, 2 * par)

                    steps(pe, step)

        with ExitStack() as c:
            te_sb = sb("te_sb", [1, 6 * P], I32, c)
            xs = sb("xs", [P, BUF, TB, C], F32, c)
            we = sb("we", [P, BUF, TB, P], F32, c)
            xsT = sb("xsT", [P, 2, TB * P], F32, c)
            sg = sb("sg", [P, 2, TB * P], F32, c)
            hs = sb("hs", [P, 2, TB * P], F32, c)
            ys = sb("ys", [P, BUF, TB, C], F32, c)
            ps_x = c.enter_context(nc.psum_tensor("ps_x", [P, 2, TB * P], F32))
            ps_e = c.enter_context(nc.psum_tensor("ps_e", [P, 2, TB * P], F32))
            ps_z = c.enter_context(nc.psum_tensor("ps_z", [P, 2, 2, 512], F32))
            te_in = sem("te_in")
            rows_loaded = [sem(f"rows_loaded{u}") for u in range(BUF)]
            experts_loaded = [sem(f"experts_loaded{u}") for u in range(BUF)]
            experts_loaded_pool = [sem(f"experts_loaded_pool{u}") for u in range(BUF)]
            ys_stored = [sem(f"ys_stored{u}") for u in range(BUF)]
            rows_turned, rows_copied, up_done = sem("rows_turned"), sem("rows_copied"), sem("up_done")
            gate_done, hidden_done, down_done = sem("gate_done"), sem("hidden_done"), sem("down_done")
            ys_ready = sem("ys_ready")
            with nc.Block() as block:
                def slot_rows(t, n):
                    return t[bass.ds(n * TB * P, TB * P), :].rearrange("(i p) c -> p i c", p=P)

                def batches(e, stages):
                    def step(k, u):
                        for lag, stage in stages:
                            kk, uu = (k, u - lag) if u >= lag else (k - 1, u - lag + BUF)
                            if some(kk + 1) and some(NBATCH // BUF - kk if isinstance(kk, int) else 1):
                                stage(BUF * kk + uu, kk, uu)

                    for u in range(BUF):
                        step(0, u)
                    with e.Fori(1, NBATCH // BUF) as k:
                        for u in range(BUF):
                            step(k, u)
                    for u in range(max(lag for lag, _ in stages)):
                        step(NBATCH // BUF, u)

                def load_experts(e, loaded_by, n, k, u, tiles):
                    if some(n - (BUF - 1)):
                        e.wait_ge(down_done, n - (BUF - 1))
                        e.sem_inc(held, 1)
                    for i in tiles:
                        row = e.value_load(te_sb[0:1, bass.ds(n * TB + i, 1)], min_val=0, max_val=NE - 1)
                        e.dma_start(we[:, u, i, :], w_expert[bass.ds(row, 1)].rearrange("e p f -> p (e f)"))\
                            .then_inc(loaded_by[u], 16)

                @block.sync
                def _(sp):
                    sp.dma_start(te_sb[:], tile_expert_dram).then_inc(te_in, 16)
                    sp.wait_ge(te_in, 16)

                    def load(n, k, u):
                        if some(n - (BUF - 1)):
                            sp.wait_ge(rows_turned, n - (BUF - 1))
                        sp.dma_start(xs[:, u], slot_rows(xslot_dram, n)).then_inc(rows_loaded[u], 16)
                        load_experts(sp, experts_loaded, n, k, u, (0, 1))

                    batches(sp, [(0, load)])

                @block.tensor
                def _(pe):
                    def turn(n, k, u):
                        pe.wait_ge(rows_loaded[u], 16 * k + 16)
                        if some(n - 1):
                            pe.wait_ge(rows_copied, n - 1)
                        for i in range(TB):
                            last = pe.transpose(ps_x[:, u % 2, i * P:(i + 1) * P], xs[:, u, i, :], ident[:])
                        last.then_inc(rows_turned, 1)

                    def up(n, k, u):
                        pe.wait_ge(experts_loaded[u], 16 * (TB - 1) * (k + 1))
                        pe.wait_ge(experts_loaded_pool[u], 16 * (k + 1))
                        pe.wait_ge(rows_copied, n + 1)
                        if some(n - 1):
                            pe.wait_ge(hidden_done, n - 1)
                        for i in range(TB):
                            for half in range(2):
                                last = pe.matmul(ps_e[half * I:(half + 1) * I, u % 2, i * P:(i + 1) * P],
                                                 we[:, u, i, 0:I], xsT[:, u % 2, i * P:(i + 1) * P],
                                                 start=True, stop=True)
                        last.then_inc(up_done, 1)

                    def down(n, k, u):
                        pe.wait_ge(hidden_done, n + 1)
                        if some(n - 1):
                            pe.wait_ge(ys_ready, n - 1)
                        for i in range(TB):
                            for half in range(2):
                                rows = slice(half * I, (half + 1) * I)
                                last = pe.matmul(ps_z[:, u % 2, half, i * I:(i + 1) * I],
                                                 hs[rows, u % 2, i * P:(i + 1) * P], we[rows, u, i, I:2 * I],
                                                 start=True, stop=True)
                        last.then_inc(down_done, 1)

                    batches(pe, [(0, turn), (1, up), (2, down)])

                @block.scalar
                def _(act):
                    def copy_rows(n, k, u):
                        act.wait_ge(rows_turned, n + 1)
                        if some(n - 1):
                            act.wait_ge(up_done, n - 1)
                        act.activation(xsT[:, u % 2], ps_x[:, u % 2], ACT.Copy).then_inc(rows_copied, 1)

                    def gate(n, k, u):
                        act.wait_ge(up_done, n + 1)
                        if some(n - 1):
                            act.wait_ge(hidden_done, n - 1)
                        act.activation(sg[:, u % 2], ps_e[:, u % 2], ACT.Sigmoid).then_inc(gate_done, 1)

                    def load(n, k, u):
                        load_experts(act, experts_loaded, n, k, u, (2,))

                    act.wait_ge(te_in, 16)
                    batches(act, [(0, load), (3, copy_rows), (4, gate)])

                @block.vector
                def _(dve):
                    def hidden(n, k, u):
                        dve.wait_ge(gate_done, n + 1)
                        if some(n - 1):
                            dve.wait_ge(down_done, n - 1)
                        dve.tensor_tensor(hs[:, u % 2], sg[:, u % 2], ps_e[:, u % 2], ALU.mult).then_inc(hidden_done, 1)

                    def copy_out(n, k, u):
                        dve.wait_ge(down_done, n + 1)
                        if some(16 * k):
                            dve.wait_ge(ys_stored[u], 16 * k)
                        dve.tensor_copy(ys[:, u].rearrange("p i (h c) -> p h i c", h=2),
                                        ps_z[:, u % 2, :, 0:TB * I].rearrange("p h (i c) -> p h i c", i=TB))\
                            .then_inc(ys_ready, 1)

                    batches(dve, [(0, hidden), (1, copy_out)])

                @block.gpsimd
                def _(pool):
                    def store(n, k, u):
                        pool.wait_ge(ys_ready, n + 1)
                        pool.dma_start(slot_rows(yslot_dram, n), ys[:, u]).then_inc(ys_stored[u], 16)

                    def load(n, k, u):
                        load_experts(pool, experts_loaded_pool, n, k, u, (3,))

                    pool.wait_ge(te_in, 16)
                    batches(pool, [(0, load), (6, store)])
                    for u in range(BUF):
                        pool.wait_ge(ys_stored[u], 16 * (NBATCH // BUF))

        with ExitStack() as c:
            NS = J * TOPK
            yg = sb("yg", [P, NS, C], F32, c)
            si = sb("si", [P, NS], U32, c)
            gt = sb("gt", [P, NS], F32, c)
            acc = sb("acc", [P, 2, J, C], F32, c)
            base_in = [sem(f"base_in{u}") for u in range(2)]
            slots_here, gathered, summed, chain = sem("slots_here"), sem("gathered"), sem("summed"), sem("chain")
            out_stored = [sem(f"out_stored{u}") for u in range(2)]
            with nc.Block() as block:
                @block.sync
                def _(sp):
                    def body(k):
                        for u in range(2):
                            it = k * 2 + u
                            if some(16 * k):
                                sp.wait_ge(out_stored[u], 16 * k)
                            sp.dma_start(acc[:, u], chunk_rows(attn_dram, it)).then_inc(base_in[u], 16)
                            sp.wait_ge(summed, it + 1)
                            sp.dma_start(chunk_rows(out_rows, it), acc[:, u]).then_inc(out_stored[u], 16)
                    peeled(sp, NCH // 2, body)
                    for u in range(2):
                        sp.wait_ge(out_stored[u], 16 * (NCH // 2))

                @block.gpsimd
                def _(pool):
                    def body(it):
                        pool.wait_ge(slots_here, it + 1)
                        pool.sem_inc(held, 1)
                        for n in range(NS):
                            pool.indirect_dma_start(yg[:, n, :], None, yslot_dram,
                                                    bass.IndirectOffsetOnAxis(ap=si[:, n:n + 1], axis=0))\
                                .then_inc(gathered, 16)
                    peeled(pool, NCH, body)
                @block.vector
                def _(dve):
                    def body(k):
                        for u in range(2):
                            it = k * 2 + u
                            dve.tensor_copy(gt[:], gates_all[:, bass.ds(it * NS, NS)]).then_inc(chain, 1)
                            dve.tensor_copy(si[:], slots_all[:, bass.ds(it * NS, NS)]).then_inc(slots_here, 1)
                            dve.wait_ge(base_in[u], 16 * k + 16)
                            dve.wait_ge(gathered, 16 * NS * it + 16 * NS)
                            dve.wait_ge(chain, (1 + TOPK) * it + 1)
                            for kk in range(TOPK):
                                for j in range(J):
                                    n = j * TOPK + kk
                                    last = dve.scalar_tensor_tensor(
                                        out=acc[:, u, j, :], in0=yg[:, n, :], scalar=gt[:, n:n + 1],
                                        in1=acc[:, u, j, :], op0=ALU.mult, op1=ALU.add)
                                last.then_inc(chain, 1)
                                if some((1 + TOPK) * it + 2 + kk):
                                    dve.wait_ge(chain, (1 + TOPK) * it + 2 + kk)
                            dve.sem_inc(summed, 1)
                    peeled(dve, NCH // 2, body)
_OUT = ((8, 1024, 128), "float32")


def kernel(**inputs):
    import numpy as _np
    import concourse.bacc as _bacc
    from concourse import mybir as _mybir
    from concourse.bass_utils import run_bass_kernel_spmd as _run

    a = {k.replace("L0_", ""): _np.asarray(v) for k, v in inputs.items()}
    heads = 8
    wg = a["ffn_w_gate"].transpose(0, 2, 1)
    wd = a["ffn_w_down"].transpose(0, 2, 1)
    half = wd.shape[2] // 2
    wd = _np.concatenate([wd[:, :, :half], wd[:, :, half:]], axis=1)
    laid = {
        "x": a["attn_x"],
        "w_dispT": a["attn_W_disp"].T,
        "w_val": a["attn_W_val"],
        "relT": a["attn_rel_pos_emb"].T,
        "w_strain": _np.tile(a["attn_W_strain"], (heads, 1)),
        "w_pos": _np.tile(a["attn_W_pos"], (1, heads)),
        "w_bond": _np.tile(a["attn_W_bond"], (heads, 1)),
        "w_dmg": _np.tile(a["attn_W_dmg"], (heads, 1)),
        "b_dmg": _np.tile(a["attn_b_dmg"][:, None], (heads, 1)),
        "w_dmg_out": _np.tile(a["attn_W_dmg_out"], (heads, 1)),
        "b_dmg_out": _np.tile(a["attn_b_dmg_out"][:, None], (128, 1)),
        "w_cproj": a["attn_W_cproj"],
        "router_wT": a["ffn_router_w"].T,
        "expert_bias": a["ffn_expert_bias"],
        "w_expert": _np.concatenate([wg, wd], axis=2),
        "w_gate_sharedT": a["ffn_w_gate_shared"].T,
        "w_down_sharedT": a["ffn_w_down_shared"].T,
    }
    nc = _bacc.Bacc("TRN2", target_bir_lowering=False, num_devices=1)
    arrays, args = {}, []
    for name, v in laid.items():
        arrays[f"in_{name}"] = _np.ascontiguousarray(v)
        args.append(nc.dram_tensor(f"in_{name}", v.shape, _mybir.dt.from_np(v.dtype), kind="ExternalInput").ap())
    args.append(nc.dram_tensor("out_0", _OUT[0], _mybir.dt.from_np(_np.dtype(_OUT[1])), kind="ExternalOutput").ap())
    moe_attention_layer(nc, *args)
    r = _run(nc, [arrays], core_ids=[0])
    return r.results[0]["out_0"]
```

```python
from contextlib import ExitStack

import concourse.bass as bass
from concourse import mybir

F32 = mybir.dt.float32
BF16 = mybir.dt.bfloat16
I32 = mybir.dt.int32
U32 = mybir.dt.uint32
ALU = mybir.AluOpType
ACT = mybir.ActivationFunctionType
AX = mybir.AxisListType

P = 128
NEG = -1.0e30
LN_EPS = 1e-5
GATE_EPS = 1e-9
ROUTED_SCALE = 2.5
FAR = -1.0e9
TOPK = 8
POOL_ITEMS = (3,)
BIASED = (6, 14)


def moe_attention_layer(nc, x, w_dispT, w_val, relT, w_strain, w_pos, w_bond, w_dmg, b_dmg,
                        w_dmg_out, b_dmg_out, w_cproj, router_wT, expert_bias, w_expert,
                        w_gate_sharedT, w_down_sharedT, out):
    B, T, C = x.shape
    D, E = relT.shape[1], relT.shape[0]
    H = w_dispT.shape[0] // E
    HS = C // H
    NE = router_wT.shape[1]
    I = w_gate_sharedT.shape[1]
    HG = 2
    HH = H // HG
    TC = 512
    CB = T // TC
    NCH = B * CB
    J = TC // P
    NBLK = NCH * J
    NTOK = B * T
    PAD = D
    SW = TC + PAD
    NTILE = NTOK * TOPK // P + NE
    NSLOT = NTILE * P
    TB = 4
    NBATCH = NTILE // TB
    ZR = NSLOT // NCH // P
    BUF = 8
    BANDW = P * HH
    HALF = P // 2
    assert C == P and HH * E == P and D == HALF and NTILE % (BUF * TB) == 0

    with ExitStack() as ctx:
        def dram(name, shape, dt=F32):
            return nc.dram_tensor(name, shape, dt).ap()

        def sem(name):
            return ctx.enter_context(nc.semaphore(name))

        s_dram = dram("s_dram", (2 * HG, B, P, PAD + T))
        val_dram = dram("val_dram", (B, PAD + T + PAD, C))
        xn_dram = dram("xn_dram", (NTOK, C))
        rank_dram = dram("rank_dram", (NTOK, NE))
        part_dram = dram("part_dram", (NTOK, C))
        band_dram = dram("band_dram", (2, J, P, BANDW))
        mask_dram = dram("mask_dram", (CB, P, D))
        tile_expert_dram = dram("tile_expert_dram", (1, 6 * P), I32)
        xslot_dram = dram("xslot_dram", (NSLOT, C))
        yslot_dram = dram("yslot_dram", (NSLOT, C))
        x_rows = x.rearrange("b t c -> (b t) c")
        out_rows = out.rearrange("b t c -> (b t) c")

        def chunk_rows(t, it):
            return t[bass.ds(it * TC, TC), :].rearrange("(j p) c -> p j c", p=P)

        held = sem("held")

        def some(n):
            return not isinstance(n, int) or n > 0

        def peeled(e, n, body):
            body(0)
            with e.Fori(1, n) as i:
                body(i)

        def ahead(e, n, body):
            body(0)
            with e.Fori(1, n - 1) as i:
                body(i)
            body(n - 1, last=True)

        def sb(name, shape, dt=F32, c=ctx):
            return c.enter_context(nc.sbuf_tensor(name, shape, dt))

        ident = sb("ident", [P, P])
        gates_all = sb("gates_all", [P, NBLK * TOPK])
        slots_all = sb("slots_all", [P, NBLK * TOPK], U32)
        w1 = sb("w1", [P, 2 * HG, P])
        wval_sb = sb("wval_sb", [P, C])
        wr_sb = sb("wr_sb", [P, NE])
        bias_sb = sb("bias_sb", [P, NE])
        wgs_sb = sb("wgs_sb", [P, I])
        wds_sb = sb("wds_sb", [I, C])
        wc_sb = sb("wc_sb", [P, C])
        rpos = sb("rpos", [P, D])
        bdmg_sb = sb("bdmg_sb", [P, 1])
        hbout = sb("hbout", [P, 1])
        wsel = sb("wsel", [P, 2, 4, 32])
        tri = sb("tri", [P, P], BF16)
        ones = sb("ones", [P, P], BF16)
        carry = sb("carry", [P, NE])
        iota_e = sb("iota_e", [P, NE])
        tile_id = sb("tile_id", [P, 6])
        mhalf = sb("mhalf", [P, J])

        zero = sb("zero", [P, 2048])
        slots_zeroed = sem("slots_zeroed")

        with ExitStack() as c:
            mask_sb = sb("mask_sb", [P, D], F32, c)
            bm = sb("bm", [P, HH], F32, c)
            wdT = sb("wdT", [P, HG, C], F32, c)
            bd = sb("bd", [P, 2, P], F32, c)
            wst = sb("wst", [P, 2, E], F32, c)
            wcol = sb("wcol", [P, 2], F32, c)
            wpos_sb = sb("wpos_sb", [E, P], F32, c)
            rel_sb = sb("rel_sb", [E, D], F32, c)
            bout_sb = sb("bout_sb", [P, 1], F32, c)
            psw = c.enter_context(nc.psum_tensor("psw", [P, 5, 512], F32))
            loaded = sem("const_loaded")
            zeroed = sem("const_zeroed")
            filled = sem("const_filled")
            pool_step = sem("const_pool_step")
            blockmask_ready = sem("blockmask_ready")
            bd_ready = sem("bd_ready")
            w1_done = sem("w1_done")
            with nc.Block() as block:
                @block.sync
                def _(sp):
                    for dst, src in ((wdT[:], w_dispT.rearrange("(g p) c -> p g c", p=P)), (wval_sb[:], w_val),
                                     (wst[:, 0, :], w_strain), (wst[:, 1, :], w_dmg), (wcol[:, 0:1], w_bond),
                                     (wcol[:, 1:2], w_dmg_out), (wpos_sb[:], w_pos), (rel_sb[:], relT),
                                     (bout_sb[:], b_dmg_out), (bdmg_sb[:], b_dmg), (wr_sb[:], router_wT),
                                     (wgs_sb[:], w_gate_sharedT), (wds_sb[:], w_down_sharedT),
                                     (wc_sb[:], w_cproj), (bias_sb[:], expert_bias.partition_broadcast(P))):
                        sp.dma_start(dst, src).then_inc(loaded, 16)
                    sp.wait_ge(zeroed, 1)
                    sp.dma_start(band_dram.rearrange("s j p f -> p (s j) f"),
                                 zero[:, 0:BANDW].unsqueeze(1).to_broadcast([P, 2 * J, BANDW])).then_inc(filled, 16)
                    for i in range(2 * HG):
                        sp.dma_start(s_dram[i, :, :, 0:PAD].rearrange("b p t -> p b t"),
                                     zero[:, 0:B * PAD].rearrange("p (b t) -> p b t", b=B)).then_inc(filled, 16)
                    for lo in (0, PAD + T):
                        sp.dma_start(val_dram[:, lo:lo + PAD, :].rearrange("b p c -> p b c"),
                                     zero[0:PAD, 0:B * C].rearrange("p (b c) -> p b c", b=B)).then_inc(filled, 16)
                    sp.dma_start(mask_dram[1:CB].rearrange("n p d -> p n d"),
                                 zero[:, 0:(CB - 1) * D].rearrange("p (n d) -> p n d", n=CB - 1)).then_inc(filled, 16)
                    sp.wait_ge(pool_step, 6)
                    sp.dma_start(mask_dram[0], mask_sb[:]).then_inc(filled, 16)
                    sp.wait_ge(filled, 16 * (1 + 2 * HG + 2 + 2))

                @block.gpsimd
                def _(pool):
                    pool.memset(bm[:], 1.0).then_inc(pool_step, 1)
                    pool.wait_ge(pool_step, 1)
                    pool.affine_select(out=bm[:], in_=bm[:], compare_op=ALU.is_ge, fill=0.0, base=0,
                                       pattern=[[-E, HH]], channel_multiplier=1).then_inc(pool_step, 1)
                    pool.wait_ge(pool_step, 2)
                    pool.affine_select(out=bm[:], in_=bm[:], compare_op=ALU.is_ge, fill=0.0, base=E - 1,
                                       pattern=[[E, HH]], channel_multiplier=-1).then_inc(blockmask_ready, 1)
                    pool.memset(ident[:], 0.0).then_inc(pool_step, 1)
                    pool.memset(mask_sb[:], 0.0).then_inc(pool_step, 1)
                    pool.memset(tri[:], 1.0)
                    pool.memset(ones[:], 1.0)
                    pool.memset(mhalf[:], -0.5).then_inc(pool_step, 1)
                    pool.wait_ge(pool_step, 5)
                    pool.affine_select(out=mask_sb[:], in_=mask_sb[:], compare_op=ALU.is_ge, fill=NEG,
                                       base=-(D - 1), pattern=[[1, D]], channel_multiplier=1).then_inc(pool_step, 1)
                    pool.affine_select(out=ident[:], in_=ident[:], compare_op=ALU.not_equal, fill=1.0, base=0,
                                       pattern=[[-1, P]], channel_multiplier=1)
                    pool.affine_select(out=tri[:], in_=tri[:], compare_op=ALU.is_gt, fill=0.0, base=0,
                                       pattern=[[1, P]], channel_multiplier=-1)
                    pool.iota(iota_e[:], pattern=[[1, NE]], base=0, channel_multiplier=0,
                              allow_small_or_imprecise_dtypes=True)
                    pool.iota(tile_id[:], pattern=[[P, 6]], base=0, channel_multiplier=1,
                              allow_small_or_imprecise_dtypes=True).then_inc(pool_step, 1)

                @block.vector
                def _(dve):
                    dve.memset(zero[:], 0.0).then_inc(zeroed, 1)
                    dve.memset(wsel[:], 0.0).then_inc(zeroed, 1)
                    dve.memset(carry[:], 0.0)
                    dve.wait_ge(loaded, 16 * 15)
                    dve.wait_ge(blockmask_ready, 1)
                    dve.wait_ge(zeroed, 2)
                    for ty in range(2):
                        for h in range(HH):
                            last = dve.tensor_scalar(bd[:, ty, h * E:(h + 1) * E], wst[:, ty, :], bm[:, h:h + 1],
                                                     None, ALU.mult)
                        last.then_inc(bd_ready, 1)
                        for q in range(4):
                            dve.tensor_scalar(wsel[:, ty, q, HH * q:HH * (q + 1)], bm[:], wcol[:, ty:ty + 1],
                                              None, ALU.mult)
                    dve.tensor_scalar(hbout[:], bout_sb[:], 0.5, None, ALU.mult)
                    dve.wait_ge(w1_done, 1)
                    for i in range(2 * HG):
                        dve.tensor_copy(w1[:, i, :], psw[:, i, 0:P])
                    dve.tensor_copy(rpos[:], psw[:, 4, 0:D])

                @block.tensor
                def _(pe):
                    pe.wait_ge(loaded, 16 * 15)
                    for ty in range(2):
                        pe.wait_ge(bd_ready, ty + 1)
                        for g in range(HG):
                            pe.matmul(psw[:, ty * HG + g, 0:P], wdT[:, g, :], bd[:, ty, :], start=True, stop=True)
                    pe.matmul(psw[:, 4, 0:D], wpos_sb[:], rel_sb[:], start=True, stop=True).then_inc(w1_done, 1)

        with ExitStack() as c:
            xin = sb("xin", [P, 2, J, C], F32, c)
            xn = sb("xn", [P, J, C], F32, c)
            xT = sb("xT", [P, TC], F32, c)
            st6 = sb("st6", [P, J, 6], F32, c)
            mv = sb("mv", [P, J, 2], F32, c)
            ve = sb("ve", [P, J], F32, c)
            rstd = sb("rstd", [P, J], F32, c)
            s_sb = sb("s_sb", [P, 2 * HG, TC], F32, c)
            v_sb = sb("v_sb", [P, J, C], F32, c)
            probs = sb("probs", [P, J, NE], F32, c)
            sig_h = sb("sig_h", [I, TC], F32, c)
            act_h = sb("act_h", [I, TC], F32, c)
            part_sb = sb("part_sb", [P, J, C], F32, c)
            top = sb("top", [P, J, TOPK], F32, c)
            topi = sb("topi", [P, J, TOPK], U32, c)
            left = sb("left", [P, J, NE], F32, c)
            chosen = sb("chosen", [P, J, NE], BF16, c)
            gsum = sb("gsum", [P, J], F32, c)
            ginv = sb("ginv", [P, J], F32, c)
            rank_sb = sb("rank_sb", [P, J, NE], F32, c)
            unchosen = sb("unchosen", [P, J, NE], F32, c)
            expert = sb("expert", [P, J, TOPK], F32, c)
            pairs = sb("pairs", [P, J, TOPK, TOPK], F32, c)
            place = sb("place", [P, J, TOPK], F32, c)
            ps_t = c.enter_context(nc.psum_tensor("ps_t", [P, TC], F32))
            ps_s = c.enter_context(nc.psum_tensor("ps_s", [P, 2, TC], F32))
            ps_v = c.enter_context(nc.psum_tensor("ps_v", [P, J, C], F32))
            ps_r = c.enter_context(nc.psum_tensor("ps_r", [P, 2, 512], F32))
            ps_h = c.enter_context(nc.psum_tensor("ps_h", [P, TC], F32))
            ps_y = c.enter_context(nc.psum_tensor("ps_y", [P, J, C], F32))
            x_loaded = [sem(f"x_loaded{u}") for u in range(2)]
            x_free = [sem(f"x_free{u}") for u in range(2)]
            var_ready, rstd_ready, xn_ready = sem("var_ready"), sem("rstd_ready"), sem("xn_ready")
            stats_ready = sem("stats_ready")
            xt_done, xt_copied = sem("xt_done"), sem("xt_copied")
            s_done, s_evac_act, s_evac_dve = sem("s_done"), sem("s_evac_act"), sem("s_evac_dve")
            v_done, v_evac = sem("v_done"), sem("v_evac")
            r_done, logits_ready, probs_ready = sem("r_done"), sem("logits_ready"), sem("probs_ready")
            h_done, sig_ready, acth_ready, y_done = sem("h_done"), sem("sig_ready"), sem("acth_ready"), sem("y_done")
            part_ready, top_step, chosen_ready = sem("part_ready"), sem("top_step"), sem("chosen_ready")
            rank_masked, unchosen_ready = sem("rank_masked"), sem("unchosen_ready")
            rank_done, rank_ready, carry_used = sem("rank_done"), sem("rank_ready"), sem("carry_used")
            stored = {n: sem(f"stored_{n}") for n in ("xn", "s", "v", "part", "rank")}

            STEPS = 3 * J + 10

            def rank_ps(j):
                return ps_r[:, j // 2, (j % 2) * NE:(j % 2 + 1) * NE]

            with nc.Block() as block:
                @block.sync
                def _(sp):
                    def load(it, u):
                        sp.dma_start(xin[:, u], chunk_rows(x_rows, it)).then_inc(x_loaded[u], 16)

                    def body(k, last=False):
                        for u in range(2):
                            it = k * 2 + u
                            if not (last and u == 1):
                                if some(k + u):
                                    sp.wait_ge(x_free[1 - u], k + u)
                                load(it + 1, 1 - u)
                            sp.wait_ge(xn_ready, J * it + J)
                            sp.dma_start(chunk_rows(xn_dram, it), xn[:]).then_inc(stored["xn"], 16)
                            sp.dma_start(xslot_dram[bass.ds(it * ZR * P, ZR * P), :]
                                         .rearrange("(p n r) c -> p n (r c)", p=P, n=3),
                                         zero[:, 0:ZR * C // 3].unsqueeze(1).to_broadcast([P, 3, ZR * C // 3]))\
                                .then_inc(slots_zeroed, 16)
                            sp.wait_ge(part_ready, it + 1)
                            sp.dma_start(chunk_rows(part_dram, it), part_sb[:]).then_inc(stored["part"], 16)

                    load(0, 0)
                    ahead(sp, NCH // 2, body)
                    for s in stored.values():
                        sp.wait_ge(s, 16 * NCH)

                @block.gpsimd
                def _(pool):
                    def root(it):
                        pool.wait_ge(var_ready, it + 1)
                        pool.tensor_tensor(rstd[:], ve[:], mhalf[:], ALU.pow).then_inc(rstd_ready, 1)

                    def chunk(b, tc, it, last=False):
                        if not last:
                            root(it + 1)
                        pool.wait_ge(s_evac_act, 2 * it + 2)
                        pool.wait_ge(s_evac_dve, 2 * it + 2)
                        pool.dma_start(s_dram[:, bass.ds(b, 1), :, bass.ds(tc * TC + PAD, TC)]
                                       .rearrange("i b p t -> p (i b) t"), s_sb[:]).then_inc(stored["s"], 16)
                        pool.wait_ge(v_evac, it + 1)
                        pool.dma_start(val_dram[bass.ds(b, 1), bass.ds(tc * TC + PAD, TC), :]
                                       .rearrange("b (j p) c -> p (b j) c", p=P), v_sb[:]).then_inc(stored["v"], 16)
                        pool.wait_ge(unchosen_ready, it + 1)
                        pool.wait_ge(rank_ready, it + 1)
                        pool.tensor_tensor(rank_sb[:], rank_sb[:], unchosen[:], ALU.add).then_inc(rank_masked, 1)
                        pool.wait_ge(rank_masked, it + 1)
                        pool.dma_start(chunk_rows(rank_dram, it), rank_sb[:]).then_inc(stored["rank"], 16)

                    root(0)
                    for tc in range(CB):
                        chunk(0, tc, tc)
                    with pool.Fori(1, B - 1) as b:
                        with pool.Fori(0, CB) as tc:
                            chunk(b, tc, b * CB + tc)
                    for tc in range(CB):
                        chunk(B - 1, tc, (B - 1) * CB + tc, last=tc == CB - 1)

                @block.scalar
                def _(act):
                    def copy_turned(it):
                        act.wait_ge(xt_done, it + 1)
                        act.activation(xT[:], ps_t[:], ACT.Copy).then_inc(xt_copied, 1)

                    def body(it, last=False):
                        act.wait_ge(logits_ready, it + 1)
                        act.activation(probs[:], probs[:], ACT.Sigmoid).then_inc(probs_ready, 1)
                        act.wait_ge(h_done, it + 1)
                        act.activation(sig_h[:], ps_h[0:I, :], ACT.Sigmoid).then_inc(sig_ready, 1)
                        if some(16 * it):
                            act.wait_ge(stored["s"], 16 * it)
                        for i in (0, 2):
                            act.wait_ge(s_done, 4 * it + i + 1)
                            act.activation(s_sb[:, i, :], ps_s[:, 0, :], ACT.Copy).then_inc(s_evac_act, 1)
                        if not last:
                            copy_turned(it + 1)

                    copy_turned(0)
                    ahead(act, NCH, body)

                @block.tensor
                def _(pe):
                    def turn(it):
                        if some(it):
                            pe.wait_ge(xt_copied, it)
                        for j in range(J):
                            pe.wait_ge(xn_ready, J * it + j + 1)
                            t = pe.transpose(ps_t[:, j * P:(j + 1) * P], xn[:, j, :], ident[:])
                        t.then_inc(xt_done, 1)

                    def body(it, last=False):
                        final = last
                        if some(it):
                            pe.wait_ge(rank_ready, it)
                        pe.wait_ge(xt_copied, it + 1)
                        for j in range(J):
                            last = pe.matmul(rank_ps(j), xT[:, j * P:(j + 1) * P], wr_sb[:], start=True, stop=True)
                        last.then_inc(r_done, 1)
                        if some(it):
                            pe.wait_ge(acth_ready, it)
                        pe.matmul(ps_h[0:I, :], wgs_sb[:], xT[:], start=True, stop=True).then_inc(h_done, 1)
                        for i in range(4):
                            if some(2 * it + i // 2):
                                pe.wait_ge((s_evac_act, s_evac_dve)[i % 2], 2 * it + i // 2)
                            pe.matmul(ps_s[:, i % 2, :], w1[:, i, :], xT[:], start=True, stop=True).then_inc(s_done, 1)
                        if some(it):
                            pe.wait_ge(v_evac, it)
                        for j in range(J):
                            last = pe.matmul(ps_v[:, j, :], xT[:, j * P:(j + 1) * P], wval_sb[:], start=True, stop=True)
                        last.then_inc(v_done, 1)
                        pe.wait_ge(acth_ready, it + 1)
                        if some(it):
                            pe.wait_ge(part_ready, it)
                        for j in range(J):
                            last = pe.matmul(ps_y[:, j, :], act_h[:, j * P:(j + 1) * P], wds_sb[:], start=True, stop=True)
                        last.then_inc(y_done, 1)
                        pe.wait_ge(chosen_ready, it + 1)
                        for j in range(J):
                            for i in range(j + 1):
                                pe.matmul(rank_ps(j), tri[:] if i == j else ones[:], chosen[:, i, :],
                                          start=(i == 0), stop=(i == j))
                        for j in range(J):
                            last = pe.matmul(ps_h[:, 0:NE], ones[:], chosen[:, j, :], start=(j == 0), stop=(j == J - 1))
                        last.then_inc(rank_done, 1)
                        if not final:
                            turn(it + 1)

                    turn(0)
                    ahead(pe, NCH, body)

                @block.vector
                def _(dve):
                    def stats(it, loads, u):
                        if some(16 * loads):
                            dve.wait_ge(x_loaded[u], 16 * loads)
                        for j in range(J):
                            dve.bn_stats(st6[:, j, :], xin[:, u, j, :]).then_inc(stats_ready, 1)
                        dve.wait_ge(stats_ready, 2 * J * it + J)
                        dve.sem_inc(held, 1)
                        for j in range(J):
                            dve.bn_aggr(mv[:, j, :], st6[:, j, :]).then_inc(stats_ready, 1)
                        dve.wait_ge(stats_ready, 2 * J * it + 2 * J)
                        dve.tensor_scalar(ve[:], mv[:, :, 1], LN_EPS, None, ALU.add).then_inc(var_ready, 1)

                    def norm(it, u):
                        dve.wait_ge(rstd_ready, it + 1)
                        if some(16 * it):
                            dve.wait_ge(stored["xn"], 16 * it)
                        if some(it):
                            dve.wait_ge(xt_done, it)
                        for j in range(J):
                            dve.tensor_scalar(xn[:, j, :], xin[:, u, j, :], mv[:, j, 0:1], rstd[:, j:j + 1],
                                              ALU.subtract, ALU.mult).then_inc(xn_ready, 1)

                    def body(k, last=False):
                        for u in range(2):
                            it = k * 2 + u
                            more = not (last and u == 1)
                            dve.wait_ge(r_done, it + 1)
                            dve.tensor_tensor(probs[:].rearrange("p (a b) e -> p a b e", a=2),
                                              ps_r[:, :, 0:2 * NE].rearrange("p a (b e) -> p a b e", b=2),
                                              bias_sb[:].unsqueeze(1).unsqueeze(1).to_broadcast([P, 2, 2, NE]),
                                              ALU.add).then_inc(logits_ready, 1)
                            if more:
                                stats(it + 1, k + 1 + u, 1 - u)
                            dve.wait_ge(sig_ready, it + 1)
                            dve.tensor_tensor(act_h[:], sig_h[:], ps_h[0:I, :], ALU.mult).then_inc(acth_ready, 1)
                            if some(16 * it):
                                dve.wait_ge(stored["s"], 16 * it)
                            dve.wait_ge(s_done, 4 * it + 2)
                            dve.tensor_copy(s_sb[:, 1, :], ps_s[:, 1, :]).then_inc(s_evac_dve, 1)
                            dve.wait_ge(probs_ready, it + 1)
                            dve.sem_inc(held, 1)
                            for j in range(J):
                                dve.max(top[:, j, :], probs[:, j, :]).then_inc(top_step, 1)
                            dve.wait_ge(s_done, 4 * it + 4)
                            dve.tensor_copy(s_sb[:, 3, :], ps_s[:, 1, :]).then_inc(s_evac_dve, 1)
                            dve.wait_ge(top_step, STEPS * it + J)
                            dve.sem_inc(held, 1)
                            for j in range(J):
                                dve.max_index(topi[:, j, :], top[:, j, :], probs[:, j, :]).then_inc(top_step, 1)
                            for j in range(J):
                                dve.match_replace(left[:, j, :], top[:, j, :], probs[:, j, :], -1.0).then_inc(top_step, 1)
                            dve.wait_ge(v_done, it + 1)
                            if some(16 * it):
                                dve.wait_ge(stored["v"], 16 * it)
                            dve.tensor_copy(v_sb[:], ps_v[:]).then_inc(v_evac, 1)
                            if some(STEPS * it + 3 * J):
                                dve.wait_ge(top_step, STEPS * it + 3 * J)
                            dve.tensor_scalar(chosen[:], left[:], 0.0, None, ALU.is_lt).then_inc(chosen_ready, 1)
                            if some(it):
                                dve.wait_ge(rank_masked, it)
                            dve.tensor_scalar(unchosen[:], left[:], 0.0, FAR, ALU.is_ge, ALU.mult)\
                                .then_inc(unchosen_ready, 1)
                            if more:
                                norm(it + 1, 1 - u)
                            dve.wait_ge(rank_done, it + 1)
                            if some(16 * it):
                                dve.wait_ge(stored["rank"], 16 * it)
                            dve.tensor_tensor(rank_sb[:].rearrange("p (a b) e -> p a b e", a=2),
                                              ps_r[:, :, 0:2 * NE].rearrange("p a (b e) -> p a b e", b=2),
                                              carry[:].unsqueeze(1).unsqueeze(1).to_broadcast([P, 2, 2, NE]), ALU.add)\
                                .then_inc(carry_used, 1)
                            dve.wait_ge(carry_used, it + 1)
                            dve.tensor_tensor(carry[:], carry[:], ps_h[:, 0:NE], ALU.add).then_inc(rank_ready, 1)
                            dve.wait_ge(rank_ready, it + 1)
                            dve.wait_ge(y_done, it + 1)
                            if some(16 * it):
                                dve.wait_ge(stored["part"], 16 * it)
                            dve.tensor_tensor(part_sb[:], ps_y[:], xin[:, u], ALU.add).then_inc(part_ready, 1)
                            dve.wait_ge(part_ready, it + 1)
                            dve.sem_inc(x_free[u], 1)
                            dve.tensor_reduce(gsum[:], top[:], AX.X, ALU.add).then_inc(top_step, 1)
                            dve.wait_ge(top_step, STEPS * it + 3 * J + 1)
                            dve.tensor_scalar(gsum[:], gsum[:], GATE_EPS, None, ALU.add).then_inc(top_step, 1)
                            dve.wait_ge(top_step, STEPS * it + 3 * J + 2)
                            dve.reciprocal(ginv[:], gsum[:]).then_inc(top_step, 1)
                            dve.tensor_copy(expert[:], topi[:]).then_inc(top_step, 1)
                            dve.wait_ge(top_step, STEPS * it + 3 * J + 4)
                            dve.tensor_tensor(top[:], top[:], ginv[:].unsqueeze(2).to_broadcast([P, J, TOPK]),
                                              ALU.mult).then_inc(top_step, 1)
                            dve.tensor_tensor(pairs[:], expert[:].unsqueeze(2).to_broadcast([P, J, TOPK, TOPK]),
                                              expert[:].unsqueeze(3).to_broadcast([P, J, TOPK, TOPK]),
                                              ALU.is_gt).then_inc(top_step, 1)
                            dve.wait_ge(top_step, STEPS * it + 3 * J + 6)
                            dve.tensor_reduce(place[:], pairs[:], AX.X, ALU.add).then_inc(top_step, 1)
                            dve.wait_ge(top_step, STEPS * it + 3 * J + 7)
                            dve.tensor_tensor(pairs[:], place[:].unsqueeze(2).to_broadcast([P, J, TOPK, TOPK]),
                                              iota_e[:, 0:TOPK].unsqueeze(1).unsqueeze(3).to_broadcast([P, J, TOPK, TOPK]),
                                              ALU.is_equal).then_inc(top_step, 1)
                            dve.wait_ge(top_step, STEPS * it + 3 * J + 8)
                            dve.tensor_tensor(pairs[:], pairs[:], top[:].unsqueeze(2).to_broadcast([P, J, TOPK, TOPK]),
                                              ALU.mult).then_inc(top_step, 1)
                            dve.wait_ge(top_step, STEPS * it + 3 * J + 9)
                            dve.tensor_reduce(place[:], pairs[:], AX.X, ALU.add).then_inc(top_step, 1)
                            if some(STEPS * it + STEPS):
                                dve.wait_ge(top_step, STEPS * it + STEPS)
                            dve.tensor_scalar(gates_all[:, bass.ds(it * J * TOPK, J * TOPK)],
                                              place[:].rearrange("p j k -> p (j k)"), ROUTED_SCALE, None, ALU.mult)

                    stats(0, 1, 0)
                    norm(0, 0)
                    ahead(dve, NCH // 2, body)
        with ExitStack() as c:
            ci = sb("ci", [P, NE], I32, c)
            ntl = sb("ntl", [P, NE], F32, c)
            cum = [sb(f"cum{i}", [P, NE], F32, c) for i in range(2)]
            le = sb("le", [P, 6, NE], F32, c)
            tef = sb("tef", [P, 6], F32, c)
            tei = sb("tei", [P, 6], I32, c)
            place_step, tiles_known = sem("place_step"), sem("tiles_known")
            te_stored = sem("te_stored")
            with nc.Block() as block:
                @block.vector
                def _(dve):
                    n = 0

                    def then(ins):
                        nonlocal n
                        n += 1
                        ins.then_inc(place_step, 1)
                        if some(n):
                            dve.wait_ge(place_step, n)

                    then(dve.tensor_scalar(ci[:], carry[:], float(P - 1), None, ALU.add))
                    then(dve.tensor_scalar(ci[:], ci[:], 7, None, ALU.logical_shift_right))
                    then(dve.tensor_copy(ntl[:], ci[:]))
                    src, s = ntl, 1
                    i = 0
                    while s < NE:
                        dst = cum[i % 2]
                        dve.tensor_copy(dst[:, 0:s], src[:, 0:s])
                        then(dve.tensor_tensor(dst[:, s:NE], src[:, s:NE], src[:, 0:NE - s], ALU.add))
                        src, s, i = dst, 2 * s, i + 1
                    for g in range(6):
                        last = dve.tensor_scalar(le[:, g, :], src[:], tile_id[:, g:g + 1], None, ALU.is_le)
                    then(last)
                    then(dve.tensor_reduce(tef[:], le[:], AX.X, ALU.add))
                    then(dve.tensor_scalar(tei[:], tef[:], float(NE - 1), None, ALU.min))
                    dve.sem_inc(tiles_known, 1)
                    then(dve.tensor_tensor(carry[:], src[:], ntl[:], ALU.subtract))
                    then(dve.tensor_scalar(carry[:], carry[:], float(P), None, ALU.mult))

                @block.sync
                def _(sp):
                    sp.wait_ge(tiles_known, 1)
                    sp.dma_start(tile_expert_dram.rearrange("o (g p) -> p (o g)", p=P), tei[:], allow_slow_non_contiguous=True)\
                        .then_inc(te_stored, 16)
                    sp.wait_ge(te_stored, 16)

        NS = J * TOPK
        with ExitStack() as c:
            rk = sb("rk", [P, 2, J, NE], F32, c)
            slotf = sb("slotf", [P, 2, NS], F32, c)
            ranks_in = [sem(f"ranks_in{u}") for u in range(2)]
            slot_step, slots_ready = sem("slot_step"), sem("slots_ready")
            with nc.Block() as block:
                @block.sync
                def _(sp):
                    def body(k):
                        for u in range(2):
                            if some(2 * (k - 1) + u + 1 if some(k) else 0):
                                sp.wait_ge(slots_ready, 2 * (k - 1) + u + 1 if some(k) else 0)
                            sp.dma_start(rk[:, u], chunk_rows(rank_dram, 2 * k + u)).then_inc(ranks_in[u], 16)
                    peeled(sp, NCH // 2, body)

                @block.vector
                def _(dve):
                    def body(k):
                        for u in range(2):
                            it = 2 * k + u
                            dve.wait_ge(ranks_in[u], 16 * k + 16)
                            if some(2 * (k - 1) + u + 1 if some(k) else 0):
                                dve.wait_ge(slots_ready, 2 * (k - 1) + u + 1 if some(k) else 0)
                            dve.tensor_tensor(rk[:, u], rk[:, u], carry[:].unsqueeze(1).to_broadcast([P, J, NE]),
                                              ALU.add).then_inc(slot_step, 1)
                            dve.wait_ge(slot_step, (1 + J) * it + 1)
                            dve.sem_inc(held, 1)
                            for j in range(J):
                                dve.max(slotf[:, u, j * TOPK:(j + 1) * TOPK], rk[:, u, j, :]).then_inc(slot_step, 1)
                            dve.wait_ge(slot_step, (1 + J) * (it + 1))
                            dve.tensor_copy(slots_all[:, bass.ds(it * NS, NS)], slotf[:, u]).then_inc(slots_ready, 1)
                    peeled(dve, NCH // 2, body)
                    dve.wait_ge(slots_ready, NCH)

        NI = 16
        CH = 4
        NSTEP = 2 * NCH
        win_loaded = [sem(f"win_loaded{g}") for g in range(HG)]
        sub_dve, sub_pool, gelu_done, item_done = sem("sub_dve"), sem("sub_pool"), sem("gelu_done"), sem("item_done")
        tanh_done, logits_in = sem("tanh_done"), sem("logits_in")
        turned, tokens_in, max_in, centred, exped = sem("turned"), sem("tokens_in"), sem("max_in"), sem("centred"), sem("exped")
        masked, sum_in, inv_in, normed = sem("masked"), sem("sum_in"), sem("inv_in"), sem("normed")
        band_out, band_in, band_turned, band_copied = sem("band_out"), sem("band_in"), sem("band_turned"), sem("band_copied")
        av_done, v_loaded, v_spread = sem("av_done"), sem("v_loaded"), sem("v_spread")
        mask_loaded, part_loaded = sem("mask_loaded"), sem("part_loaded")
        o_copied, cproj_done, y_copied = sem("o_copied"), sem("cproj_done"), sem("y_copied")
        y_ready, y_stored = sem("y_ready"), sem("y_stored")
        v_zeroed = sem("v_zeroed")
        rows_in, slots_here = sem("rows_in"), sem("slots_here")
        scattered = [sem(f"scattered{u}") for u in range(2)]
        gates_here, base_in = sem("gates_here"), sem("base_in")
        gathered = [sem(f"gathered{j}") for j in range(J)]
        sum_round, routed_stored = sem("sum_round"), sem("routed_stored")

        def attend(c, half):
            first, end = half * NSTEP // 2, (half + 1) * NSTEP // 2
            it0 = first // 2
            biased = ((), BIASED)[half]
            chunk0 = (1 - half) * NCH // 2 - it0
            u_dve = sb(f"u_dve_{half}", [P, 3, 8, TC], F32, c)
            u_pool = sb(f"u_pool_{half}", [P, 2, 8, TC], F32, c)
            s_win = sb(f"s_win_{half}", [P, HG, 2, SW], F32, c)
            tanh_sb = sb(f"tanh_sb_{half}", [P, 2, TC], F32, c)
            lg = sb(f"lg_{half}", [P, 2, CH, TC], F32, c)
            ml = sb(f"ml_{half}", [P, J, D, HH], F32, c)
            mx = sb(f"mx_{half}", [P, J, HH], F32, c)
            wsum = sb(f"wsum_{half}", [P, J, HH], F32, c)
            winv = sb(f"winv_{half}", [P, J, HH], F32, c)
            band = sb(f"band_{half}", [P, J, BANDW], F32, c)
            at_sb = sb(f"at_sb_{half}", [P, 2, 4, P], F32, c)
            v_raw = sb(f"v_raw_{half}", [P, 2 * J, C], F32, c)
            v_msk = sb(f"v_msk_{half}", [P, 2 * J, H * 32], F32, c)
            mask_t = sb(f"mask_t_{half}", [P, D], F32, c)
            oT_sb = sb(f"oT_sb_{half}", [P, TC], F32, c)
            part_t = sb(f"part_t_{half}", [P, J, C], F32, c)
            y_sb = sb(f"y_sb_{half}", [P, J, C], F32, c)
            slot_now = sb(f"slot_now_{half}", [P, 2, NS], U32, c)
            if half == 0:
                xr = sb("xr", [P, 2, J, C], F32, c)
            else:
                yg = sb("yg", [P, NS, C], F32, c)
                gate_now = sb("gate_now", [P, 2, NS], F32, c)
                acc = sb("acc", [P, 2, J, C], F32, c)
            ps_l = c.enter_context(nc.psum_tensor(f"ps_l_{half}", [P, 2, 2, TC], F32))
            ps_o = c.enter_context(nc.psum_tensor(f"ps_o_{half}", [P, TC], F32))
            ps_u = c.enter_context(nc.psum_tensor(f"ps_u_{half}", [P, TC], F32))
            on_pool = POOL_ITEMS
            NP = len(on_pool)
            dve_of = [sum(q % 4 not in on_pool for q in range(n + 1)) for n in range(NI)]
            pool_of = [n + 1 - dve_of[n] for n in range(NI)]
            ND, NPI = dve_of[-1], pool_of[-1]

            def steps(e, step):
                for s, st in enumerate(("i", "is", "isa", "isat"), first):
                    step(s, s // 2, s % 2, st)
                with e.Fori(it0 + 2, it0 + NCH // 2) as it:
                    for par in range(2):
                        step(it * 2 + par, it, par, "isat")
                for s, st in enumerate(("sat", "at", "t"), end):
                    step(s, s // 2, s % 2, st)

            def offsets(n):
                return n // 4, 16 * (n // 4) + 8 * (n % 4 // 2), n % 2

            def windows(par, ty, d0, nd):
                row = s_win[:, par, ty, d0 + 1:d0 + 1 + TC]
                return bass.AP(row.tensor, row.offset, [list(row.ap[0]), [1, nd], [1, TC]])

            def item_buffer(n):
                if n % 4 in on_pool:
                    return u_pool[:, (pool_of[n] - 1) % 2]
                return u_dve[:, (n % 4 - sum(q < n % 4 for q in on_pool))]

            def buffer_free(n):
                if n % 4 in on_pool:
                    return n + 1 - 8 // NP
                return n - 3

            with nc.Block() as block:
                @block.sync
                def _(sp):
                    def load_windows(b, tc, it, par):
                        if some(it):
                            if some(ND * (2 * it + par - 1)):
                                sp.wait_ge(sub_dve, ND * (2 * it + par - 1))
                                sp.sem_inc(held, 1)
                            if some(NPI * (2 * it + par - 1)):
                                sp.wait_ge(sub_pool, NPI * (2 * it + par - 1))
                                sp.sem_inc(held, 1)
                        for ty in range(2):
                            sp.dma_start(s_win[:, par, ty, :],
                                         s_dram[ty * HG + par, bass.ds(b, 1), :, bass.ds(tc * TC, SW)]
                                         .rearrange("b p t -> p (b t)")).then_inc(win_loaded[par], 16)

                    def load_chunk(b, tc, it):
                        if some(2 * it):
                            sp.wait_ge(masked, 2 * it)
                        sp.dma_start(mask_t[:], mask_dram[bass.ds(tc, 1)].rearrange("n p d -> p (n d)"))\
                            .then_inc(mask_loaded, 16)
                        if some(it):
                            sp.wait_ge(v_spread, it)
                        for w in range(2 * J):
                            sp.dma_start(v_raw[:, w, :],
                                         val_dram[bass.ds(b, 1), bass.ds(tc * TC + w * HALF + 1, P), :]
                                         .rearrange("b p c -> p (b c)")).then_inc(v_loaded, 16)

                    def band_trip(u):
                        sp.wait_ge(normed, u + 1)
                        sp.sem_inc(held, 1)
                        if some(16 * u):
                            sp.wait_ge(band_in, 16 * u)
                            sp.sem_inc(held, 1)
                        for h in range(2):
                            first = band_dram[0, :, h * HALF:(h + 1) * HALF, :]
                            skewed = bass.AP(first.tensor, first.offset,
                                             [[BANDW + HH, HALF], [P * BANDW, J], [1, D * HH]])
                            sp.dma_start(skewed, ml[h * HALF:(h + 1) * HALF].rearrange("p j d h -> p j (d h)"))\
                                .then_inc(band_out, 16)
                        sp.wait_ge(band_out, 32 * u + 32)
                        sp.sem_inc(held, 1)
                        if some(8 * u):
                            sp.wait_ge(band_turned, 8 * u)
                        sp.dma_start(band[:], band_dram[0].rearrange("j p f -> p j f")).then_inc(band_in, 16)

                    def load_part(it):
                        if some(16 * it):
                            sp.wait_ge(y_stored, 16 * it)
                            sp.sem_inc(held, 1)
                        if half == 1:
                            if some(16 * (it - it0 + 1)):
                                sp.wait_ge(routed_stored, 16 * (it - it0 + 1))
                                sp.sem_inc(held, 1)
                        sp.dma_start(part_t[:], chunk_rows((part_dram, out_rows)[half], chunk0 + it))\
                            .then_inc(part_loaded, 16)

                    def store_y(it):
                        sp.wait_ge(y_ready, it + 1)
                        sp.sem_inc(held, 1)
                        sp.dma_start(chunk_rows((part_dram, out_rows)[half], chunk0 + it), y_sb[:]).then_inc(y_stored, 16)

                    def load_rows(it, par):
                        s = 2 * it + par
                        if some(16 * NS * it):
                            sp.wait_ge(scattered[par], 16 * NS * it)
                            sp.sem_inc(held, 1)
                        if some(16 * s):
                            sp.wait_ge(rows_in, 16 * s)
                            sp.sem_inc(held, 1)
                        sp.dma_start(xr[:, par], chunk_rows(xn_dram, s)).then_inc(rows_in, 16)

                    def store_routed(t, par):
                        if some(NS * (t - 1)):
                            sp.wait_ge(sum_round, NS * (t - 1))
                            sp.sem_inc(held, 1)
                        if some(16 * (t - 2)):
                            sp.wait_ge(routed_stored, 16 * (t - 2))
                            sp.sem_inc(held, 1)
                        sp.dma_start(chunk_rows(out_rows, t - 2), acc[:, par]).then_inc(routed_stored, 16)

                    def load_base(t, par):
                        if some(16 * (t - 2) if some(t - 2) else 0):
                            sp.wait_ge(routed_stored, 16 * (t - 2) if some(t - 2) else 0)
                            sp.sem_inc(held, 1)
                        if some(16 * (t - 1)):
                            sp.wait_ge(base_in, 16 * (t - 1))
                            sp.sem_inc(held, 1)
                        sp.dma_start(acc[:, 1 - par], chunk_rows(part_dram, t - 1)).then_inc(base_in, 16)

                    def routed(it, par):
                        if half == 0:
                            load_rows(it, par)
                            return
                        t = 2 * it + par - first
                        if some(t - 1):
                            store_routed(t, par)
                        if some(t):
                            load_base(t, par)

                    def chunk(b, tc, it):
                        full = some(it - it0 - 1)
                        load_windows(b, tc, it, 0)
                        routed(it, 0)
                        if some(it - it0):
                            band_trip(2 * it - 2)
                        load_windows(b, tc, it, 1)
                        if full:
                            load_part(it - 2)
                            store_y(it - 2)
                        load_chunk(b, tc, it)
                        routed(it, 1)
                        if some(it - it0):
                            band_trip(2 * it - 1)

                    b0 = (1 - half) * B // 2
                    for tc in range(CB):
                        chunk(b0, tc, it0 + tc)
                    with sp.Fori(1, B // 2) as b:
                        with sp.Fori(0, CB) as tc:
                            chunk(b + b0, tc, b * CB + tc + it0)
                    if half == 1:
                        store_routed(NCH, 0)
                        load_base(NCH, 0)
                    band_trip(end - 2)
                    load_part(it0 + NCH // 2 - 2)
                    store_y(it0 + NCH // 2 - 2)
                    band_trip(end - 1)
                    if half == 1:
                        store_routed(NCH + 1, 1)
                        sp.wait_ge(routed_stored, 16 * NCH)
                    load_part(it0 + NCH // 2 - 1)
                    store_y(it0 + NCH // 2 - 1)
                    sp.wait_ge(y_stored, 16 * (it0 + NCH // 2))

                @block.gpsimd
                def _(pool):
                    pool.memset(v_msk[:], 0.0).then_inc(v_zeroed, 1)
                    pool.wait_ge(v_zeroed, half + 1)
                    if half == 0:
                        pool.wait_ge(slots_zeroed, 16 * NCH)

                    def spread(it):
                        pool.wait_ge(v_loaded, 16 * 2 * J * (it + 1))
                        if some(16 * it):
                            pool.wait_ge(av_done, 16 * it)
                            pool.sem_inc(held, 1)
                        for w in range(2 * J):
                            dst = v_msk[:, w, 0:HS]
                            last = pool.tensor_copy(
                                bass.AP(dst.tensor, dst.offset, [list(dst.ap[0]), [4 * 32, H // 4], [32 + HS, 4], [1, HS]]),
                                v_raw[:, w, :].rearrange("p (g i e) -> p g i e", g=H // 4, i=4))
                        last.then_inc(v_spread, 1)

                    def route(s, par, j):
                        pool.wait_ge(slots_here, s + 1)
                        pool.sem_inc(held, 1)
                        if half == 0:
                            pool.wait_ge(rows_in, 16 * (s + 1))
                            pool.sem_inc(held, 1)
                            for i in range(j * TOPK, (j + 1) * TOPK):
                                pool.indirect_dma_start(
                                    xslot_dram, bass.IndirectOffsetOnAxis(ap=slot_now[:, par, i:i + 1], axis=0),
                                    xr[:, par, j, :], None).then_inc(scattered[par], 16)
                        else:
                            if some(s - first):
                                pool.wait_ge(sum_round, NS * (s - first - 1) + TOPK * (j + 1))
                                pool.sem_inc(held, 1)
                            for i in range(j * TOPK, (j + 1) * TOPK):
                                pool.indirect_dma_start(
                                    yg[:, i, :], None, yslot_dram,
                                    bass.IndirectOffsetOnAxis(ap=slot_now[:, par, i:i + 1], axis=0)).then_inc(gathered[j], 16)

                    def step(s, it, par, st):
                        for n in range(NI):
                            cgrp, d0, ty = offsets(n)
                            if "i" in st and n % 4 in on_pool:
                                if pool_of[n] == 1:
                                    pool.wait_ge(win_loaded[par], 32 * it + 32)
                                if some(NI * s + buffer_free(n)):
                                    pool.wait_ge(item_done, NI * s + buffer_free(n))
                                pool.tensor_tensor(
                                    item_buffer(n), windows(par, ty, d0, 8),
                                    s_win[:, par, ty, PAD:PAD + TC].unsqueeze(1).to_broadcast([P, 8, TC]),
                                    ALU.subtract).then_inc(sub_pool, 1)
                            if "a" in st and n == 3 and par == 0:
                                spread(it - 1)
                            if "t" in st and n == 5 and par == 0:
                                if some(it - 1):
                                    pool.wait_ge(y_copied, it - 1)
                                if some(16 * (it - 1)):
                                    pool.wait_ge(part_loaded, 16 * (it - 1))
                                pool.tensor_tensor(y_sb[:], y_sb[:], part_t[:], ALU.add).then_inc(y_ready, 1)
                            if half == 1 and "s" in st and n == 15:
                                pool.wait_ge(inv_in, s)
                                pool.tensor_tensor(ml[:], ml[:], winv[:].unsqueeze(2).to_broadcast([P, J, D, HH]),
                                                   ALU.mult).then_inc(normed, 1)
                            if "i" in st and n % 4 == 3:
                                route(s, par, n // 4)

                    steps(pool, step)
                    if half == 0:
                        for u in range(2):
                            pool.wait_ge(scattered[u], 16 * NS * (NCH // 2))

                @block.scalar
                def _(act):
                    def step(s, it, par, st):
                        for n in range(NI):
                            cgrp, d0, ty = offsets(n)
                            if "i" in st:
                                if n % 4 in on_pool:
                                    if some(NPI * s + pool_of[n]):
                                        act.wait_ge(sub_pool, NPI * s + pool_of[n])
                                else:
                                    if some(ND * s + dve_of[n]):
                                        act.wait_ge(sub_dve, ND * s + dve_of[n])
                                u = item_buffer(n)
                                if n in biased:
                                    for d in range(8):
                                        last = act.activation(u[:, d, :], u[:, d, :], ACT.Gelu,
                                                              bias=rpos[:, d0 + d:d0 + d + 1])
                                    last.then_inc(gelu_done, 1)
                                elif ty:
                                    act.activation(u, u, ACT.Gelu, bias=bdmg_sb[:]).then_inc(gelu_done, 1)
                                else:
                                    act.activation(u, u, ACT.Gelu).then_inc(gelu_done, 1)
                            if n % 4 == 1 and ("i" in st if n > 1 else "s" in st):
                                k = 4 * s + cgrp - 1
                                act.wait_ge(item_done, 4 * k + 4)
                                if some(k - 1):
                                    act.wait_ge(logits_in, k - 1)
                                act.activation(tanh_sb[:, (cgrp - 1) % 2], ps_l[:, (cgrp - 1) % 2, 1], ACT.Tanh,
                                               bias=hbout[:], scale=0.5).then_inc(tanh_done, 1)
                            if "s" in st and 5 <= n <= 8:
                                j = n - 5
                                act.wait_ge(turned, 4 * (s - 1) + j + 1)
                                if some(32 * (s - 1)):
                                    act.wait_ge(band_out, 32 * (s - 1))
                                act.activation(ml[:, j].rearrange("p d h -> p (d h)"), ps_u[:], ACT.Copy)\
                                    .then_inc(tokens_in, 1)
                            if "s" in st and n == 12:
                                if some(4 * s):
                                    act.wait_ge(centred, 4 * s)
                                act.activation(ml[:], ml[:], ACT.Exp).then_inc(exped, 1)
                            for k, u in ((n - 9, s - 2) if n >= 9 and "a" in st else (0, None),
                                         (7, s - 3) if n == 0 and "t" in st else (0, None)):
                                if u is not None:
                                    act.wait_ge(band_turned, 8 * u + k + 1)
                                    if some(8 * u + k - 1):
                                        act.wait_ge(av_done, 8 * u + k - 1)
                                    act.activation(at_sb[:, k % 2].rearrange("p i t -> p (i t)"), ps_u[:], ACT.Copy)\
                                        .then_inc(band_copied, 1)
                            if "t" in st and par == 0 and n == 2:
                                if some(8 * (s - 2)):
                                    act.wait_ge(av_done, 8 * (s - 2))
                                act.activation(oT_sb[:], ps_o[:], ACT.Copy).then_inc(o_copied, 1)
                            if "t" in st and par == 0 and n == 4:
                                if some(it - 1):
                                    act.wait_ge(cproj_done, it - 1)
                                if some(16 * (it - 2)):
                                    act.wait_ge(y_stored, 16 * (it - 2))
                                act.activation(y_sb[:].rearrange("p j c -> p (j c)"), ps_u[:], ACT.Copy)\
                                    .then_inc(y_copied, 1)

                    steps(act, step)

                @block.vector
                def _(dve):
                    def bring(s, it, par):
                        if half == 0:
                            if some(16 * NS * it):
                                dve.wait_ge(scattered[par], 16 * NS * it)
                        else:
                            if some(NS * (s - first - 1)):
                                dve.wait_ge(sum_round, NS * (s - first - 1))
                            dve.tensor_copy(gate_now[:, par], gates_all[:, bass.ds((s - first) * NS, NS)])\
                                .then_inc(gates_here, 1)
                        dve.tensor_copy(slot_now[:, par], slots_all[:, bass.ds((s - first) * NS, NS)])\
                            .then_inc(slots_here, 1)

                    def add_routed(t, old, i):
                        j = i // TOPK
                        if i == 0:
                            if some(16 * t):
                                dve.wait_ge(base_in, 16 * t)
                            if some(t):
                                dve.wait_ge(gates_here, t)
                        if i % TOPK == 0:
                            if some(16 * TOPK * t):
                                dve.wait_ge(gathered[j], 16 * TOPK * t)
                        if some(NS * (t - 1) + i):
                            dve.wait_ge(sum_round, NS * (t - 1) + i)
                        dve.scalar_tensor_tensor(
                            out=acc[:, old, j, :], in0=yg[:, i, :], scalar=gate_now[:, old, i:i + 1],
                            in1=acc[:, old, j, :], op0=ALU.mult, op1=ALU.add).then_inc(sum_round, 1)

                    def step(s, it, par, st):
                        for n in range(NI):
                            cgrp, d0, ty = offsets(n)
                            if "i" in st and n == 0:
                                bring(s, it, par)
                            sums = half == 1 and "s" in st and n % 4 == 0
                            if sums and "i" not in st:
                                for d in range(8):
                                    add_routed(s - first, 1 - par, 2 * n + d)
                            if "i" in st and n % 4 not in on_pool:
                                if dve_of[n] == 1:
                                    dve.wait_ge(win_loaded[par], 32 * it + 32)
                                if some(NI * s + buffer_free(n)):
                                    dve.wait_ge(item_done, NI * s + buffer_free(n))
                                here = s_win[:, par, ty, PAD:PAD + TC]
                                if ty or n in biased:
                                    last = dve.tensor_tensor(item_buffer(n), windows(par, ty, d0, 8),
                                                             here.unsqueeze(1).to_broadcast([P, 8, TC]), ALU.subtract)
                                else:
                                    for d in range(8):
                                        last = dve.scalar_tensor_tensor(
                                            out=item_buffer(n)[:, d, :], in0=s_win[:, par, ty, d0 + d + 1:d0 + d + 1 + TC],
                                            scalar=rpos[:, d0 + d:d0 + d + 1], in1=here, op0=ALU.add, op1=ALU.subtract)
                                        if sums:
                                            if d == 7:
                                                last.then_inc(sub_dve, 1)
                                            add_routed(s - first, 1 - par, 2 * n + d)
                                if not sums:
                                    last.then_inc(sub_dve, 1)
                            if n % 4 == 0 and ("i" in st if n > 4 else "s" in st):
                                k = 4 * s + cgrp - 2
                                dve.wait_ge(tanh_done, k + 1)
                                if n > 4:
                                    if some(4 * (s - 1)):
                                        dve.wait_ge(turned, 4 * (s - 1))
                                dve.scalar_tensor_tensor(out=lg[:, par if n > 4 else 1 - par, (cgrp - 2) % 4, :],
                                                         in0=tanh_sb[:, (cgrp - 2) % 2], scalar=-5.0,
                                                         in1=ps_l[:, (cgrp - 2) % 2, 0], op0=ALU.mult,
                                                         op1=ALU.add).then_inc(logits_in, 1)
                            if "s" in st and 8 <= n <= 11:
                                j = n - 8
                                dve.wait_ge(tokens_in, 4 * (s - 1) + j + 1)
                                if j == 0:
                                    if some(16 * ((it if par else it - 1) + 1)):
                                        dve.wait_ge(mask_loaded, 16 * ((it if par else it - 1) + 1))
                                    dve.tensor_tensor(ml[:, 0], ml[:, 0],
                                                      mask_t[:].unsqueeze(2).to_broadcast([P, D, HH]), ALU.add)\
                                        .then_inc(masked, 1)
                                    dve.wait_ge(masked, s)
                                dve.tensor_reduce(mx[:, j, :], ml[:, j].rearrange("p d h -> p h d"), AX.X, ALU.max)\
                                    .then_inc(max_in, 1)
                                dve.wait_ge(max_in, 4 * (s - 1) + j + 1)
                                dve.tensor_tensor(ml[:, j], ml[:, j], mx[:, j, :].unsqueeze(1).to_broadcast([P, D, HH]),
                                                  ALU.subtract).then_inc(centred, 1)
                            if "s" in st and n == 15:
                                dve.wait_ge(exped, s)
                                dve.tensor_reduce(wsum[:], ml[:].rearrange("p j d h -> p j h d"), AX.X, ALU.add)\
                                    .then_inc(sum_in, 1)
                                dve.wait_ge(sum_in, s)
                                dve.reciprocal(winv[:], wsum[:]).then_inc(inv_in, 1)
                                if half == 0:
                                    dve.wait_ge(inv_in, s)
                                    dve.tensor_tensor(ml[:], ml[:], winv[:].unsqueeze(2).to_broadcast([P, J, D, HH]),
                                                      ALU.mult).then_inc(normed, 1)

                    steps(dve, step)

                @block.tensor
                def _(pe):
                    def values(u, k, itu, g0):
                        j, g = k // 2, g0 + k % 2
                        if k == 0:
                            pe.wait_ge(v_spread, itu + 1)
                            if g0 == 0:
                                if some(itu):
                                    pe.wait_ge(o_copied, itu)
                        pe.wait_ge(band_copied, 8 * u + k + 1)
                        for half in range(2):
                            for i in range(4):
                                h = 4 * g + i
                                last = pe.matmul(
                                    ps_o[32 * g:32 * g + 32, j * P + half * HALF:j * P + (half + 1) * HALF],
                                    v_msk[:, 2 * j + half, 32 * h:32 * h + 32],
                                    at_sb[:, k % 2, i, half * HALF:(half + 1) * HALF],
                                    start=(i == 0), stop=(i == 3))
                        last.then_inc(av_done, 1)

                    def step(s, it, par, st):
                        for n in range(NI):
                            cgrp, d0, ty = offsets(n)
                            if "i" in st:
                                if n % 4 < 2:
                                    if some(4 * s + cgrp - 1):
                                        pe.wait_ge(logits_in, 4 * s + cgrp - 1)
                                pe.wait_ge(gelu_done, NI * s + n + 1)
                                for d in range(8):
                                    q, g = (d0 + d) % 16 // 4, d % 4
                                    last = pe.matmul(ps_l[32 * g:32 * g + 32, cgrp % 2, ty, :], wsel[:, ty, q, :],
                                                     item_buffer(n)[:, d, :], start=(q == 0), stop=(q == 3))
                                last.then_inc(item_done, 1)
                            if "t" in st and n < 2:
                                values(s - 3, 6 + n, it - 1 if par else it - 2, 2 - 2 * par)
                            if "t" in st and par == 0 and n == 3:
                                if some(it - 1):
                                    pe.wait_ge(o_copied, it - 1)
                                if some(8 * (s - 2)):
                                    pe.wait_ge(band_copied, 8 * (s - 2))
                                for j in range(J):
                                    last = pe.matmul(ps_u[:, j * P:(j + 1) * P], oT_sb[:, j * P:(j + 1) * P], wc_sb[:],
                                                     start=True, stop=True)
                                last.then_inc(cproj_done, 1)
                            if "s" in st and 4 <= n <= 7:
                                j = n - 4
                                if j == 0:
                                    if some(4 * s):
                                        pe.wait_ge(logits_in, 4 * s)
                                    if "t" in st:
                                        if some(it - 1 if par == 0 else 0):
                                            pe.wait_ge(y_copied, it - 1 if par == 0 else 0)
                                        if some(8 * (s - 2)):
                                            pe.wait_ge(band_copied, 8 * (s - 2))
                                if some(4 * (s - 1) + j):
                                    pe.wait_ge(tokens_in, 4 * (s - 1) + j)
                                for g in range(CH):
                                    last = pe.transpose(
                                        ps_u[:, P * g:P * g + P].rearrange("p (q g h) -> p g q h", g=4, h=HH),
                                        lg[:, 1 - par, g, j * P:(j + 1) * P], ident[:])
                                last.then_inc(turned, 1)
                            if "a" in st and n >= 8:
                                k = n - 8
                                if k == 0:
                                    if some(16 * (s - 1)):
                                        pe.wait_ge(band_in, 16 * (s - 1))
                                    if some(4 * s if "s" in st else 0):
                                        pe.wait_ge(tokens_in, 4 * s if "s" in st else 0)
                                    if some(it - 1 if "t" in st and par == 0 else 0):
                                        pe.wait_ge(y_copied, it - 1 if "t" in st and par == 0 else 0)
                                if some(8 * (s - 2) + k):
                                    pe.wait_ge(band_copied, 8 * (s - 2) + k)
                                for i in range(4):
                                    last = pe.transpose(ps_u[:, i * P:(i + 1) * P],
                                                        band[:, k // 2, 4 * (k % 2) + i:BANDW:HH], ident[:])
                                last.then_inc(band_turned, 1)
                                if k >= 2:
                                    values(s - 2, k - 2, it - 1, 2 * par)

                    steps(pe, step)

        with ExitStack() as c:
            attend(c, 0)

        with ExitStack() as c:
            te_sb = sb("te_sb", [1, 6 * P], I32, c)
            xs = sb("xs", [P, BUF, TB, C], F32, c)
            we = sb("we", [P, BUF, TB, P], F32, c)
            xsT = sb("xsT", [P, 2, TB * P], F32, c)
            sg = sb("sg", [P, 2, TB * P], F32, c)
            hs = sb("hs", [P, 2, TB * P], F32, c)
            ys = sb("ys", [P, BUF, TB, C], F32, c)
            ps_x = c.enter_context(nc.psum_tensor("ps_x", [P, 2, TB * P], F32))
            ps_e = c.enter_context(nc.psum_tensor("ps_e", [P, 2, TB * P], F32))
            ps_z = c.enter_context(nc.psum_tensor("ps_z", [P, 2, 2, 512], F32))
            te_in = sem("te_in")
            rows_loaded = [sem(f"rows_loaded{u}") for u in range(BUF)]
            experts_loaded = [sem(f"experts_loaded{u}") for u in range(BUF)]
            experts_loaded_pool = [sem(f"experts_loaded_pool{u}") for u in range(BUF)]
            ys_stored = [sem(f"ys_stored{u}") for u in range(BUF)]
            rows_turned, rows_copied, up_done = sem("rows_turned"), sem("rows_copied"), sem("up_done")
            gate_done, hidden_done, down_done = sem("gate_done"), sem("hidden_done"), sem("down_done")
            ys_ready = sem("ys_ready")
            with nc.Block() as block:
                def slot_rows(t, n):
                    return t[bass.ds(n * TB * P, TB * P), :].rearrange("(i p) c -> p i c", p=P)

                def batches(e, stages):
                    def step(k, u):
                        for lag, stage in stages:
                            kk, uu = (k, u - lag) if u >= lag else (k - 1, u - lag + BUF)
                            if some(kk + 1) and some(NBATCH // BUF - kk if isinstance(kk, int) else 1):
                                stage(BUF * kk + uu, kk, uu)

                    for u in range(BUF):
                        step(0, u)
                    with e.Fori(1, NBATCH // BUF) as k:
                        for u in range(BUF):
                            step(k, u)
                    for u in range(max(lag for lag, _ in stages)):
                        step(NBATCH // BUF, u)

                def load_experts(e, loaded_by, n, k, u, tiles):
                    if some(n - (BUF - 1)):
                        e.wait_ge(down_done, n - (BUF - 1))
                        e.sem_inc(held, 1)
                    for i in tiles:
                        row = e.value_load(te_sb[0:1, bass.ds(n * TB + i, 1)], min_val=0, max_val=NE - 1)
                        e.dma_start(we[:, u, i, :], w_expert[bass.ds(row, 1)].rearrange("e p f -> p (e f)"))\
                            .then_inc(loaded_by[u], 16)

                @block.sync
                def _(sp):
                    sp.dma_start(te_sb[:], tile_expert_dram).then_inc(te_in, 16)
                    sp.wait_ge(te_in, 16)

                    def load(n, k, u):
                        if some(n - (BUF - 1)):
                            sp.wait_ge(rows_turned, n - (BUF - 1))
                        sp.dma_start(xs[:, u], slot_rows(xslot_dram, n)).then_inc(rows_loaded[u], 16)
                        load_experts(sp, experts_loaded, n, k, u, (0, 1))

                    batches(sp, [(0, load)])

                @block.tensor
                def _(pe):
                    def turn(n, k, u):
                        pe.wait_ge(rows_loaded[u], 16 * k + 16)
                        if some(n - 1):
                            pe.wait_ge(rows_copied, n - 1)
                        for i in range(TB):
                            last = pe.transpose(ps_x[:, u % 2, i * P:(i + 1) * P], xs[:, u, i, :], ident[:])
                        last.then_inc(rows_turned, 1)

                    def up(n, k, u):
                        pe.wait_ge(experts_loaded[u], 16 * (TB - 1) * (k + 1))
                        pe.wait_ge(experts_loaded_pool[u], 16 * (k + 1))
                        pe.wait_ge(rows_copied, n + 1)
                        if some(n - 1):
                            pe.wait_ge(hidden_done, n - 1)
                        for i in range(TB):
                            for half in range(2):
                                last = pe.matmul(ps_e[half * I:(half + 1) * I, u % 2, i * P:(i + 1) * P],
                                                 we[:, u, i, 0:I], xsT[:, u % 2, i * P:(i + 1) * P],
                                                 start=True, stop=True)
                        last.then_inc(up_done, 1)

                    def down(n, k, u):
                        pe.wait_ge(hidden_done, n + 1)
                        if some(n - 1):
                            pe.wait_ge(ys_ready, n - 1)
                        for i in range(TB):
                            for half in range(2):
                                rows = slice(half * I, (half + 1) * I)
                                last = pe.matmul(ps_z[:, u % 2, half, i * I:(i + 1) * I],
                                                 hs[rows, u % 2, i * P:(i + 1) * P], we[rows, u, i, I:2 * I],
                                                 start=True, stop=True)
                        last.then_inc(down_done, 1)

                    batches(pe, [(0, turn), (1, up), (2, down)])

                @block.scalar
                def _(act):
                    def copy_rows(n, k, u):
                        act.wait_ge(rows_turned, n + 1)
                        if some(n - 1):
                            act.wait_ge(up_done, n - 1)
                        act.activation(xsT[:, u % 2], ps_x[:, u % 2], ACT.Copy).then_inc(rows_copied, 1)

                    def gate(n, k, u):
                        act.wait_ge(up_done, n + 1)
                        if some(n - 1):
                            act.wait_ge(hidden_done, n - 1)
                        act.activation(sg[:, u % 2], ps_e[:, u % 2], ACT.Sigmoid).then_inc(gate_done, 1)

                    def load(n, k, u):
                        load_experts(act, experts_loaded, n, k, u, (2,))

                    act.wait_ge(te_in, 16)
                    batches(act, [(0, load), (3, copy_rows), (4, gate)])

                @block.vector
                def _(dve):
                    def hidden(n, k, u):
                        dve.wait_ge(gate_done, n + 1)
                        if some(n - 1):
                            dve.wait_ge(down_done, n - 1)
                        dve.tensor_tensor(hs[:, u % 2], sg[:, u % 2], ps_e[:, u % 2], ALU.mult).then_inc(hidden_done, 1)

                    def copy_out(n, k, u):
                        dve.wait_ge(down_done, n + 1)
                        if some(16 * k):
                            dve.wait_ge(ys_stored[u], 16 * k)
                        dve.tensor_copy(ys[:, u].rearrange("p i (h c) -> p h i c", h=2),
                                        ps_z[:, u % 2, :, 0:TB * I].rearrange("p h (i c) -> p h i c", i=TB))\
                            .then_inc(ys_ready, 1)

                    batches(dve, [(0, hidden), (1, copy_out)])

                @block.gpsimd
                def _(pool):
                    def store(n, k, u):
                        pool.wait_ge(ys_ready, n + 1)
                        pool.dma_start(slot_rows(yslot_dram, n), ys[:, u]).then_inc(ys_stored[u], 16)

                    def load(n, k, u):
                        load_experts(pool, experts_loaded_pool, n, k, u, (3,))

                    pool.wait_ge(te_in, 16)
                    batches(pool, [(0, load), (6, store)])
                    for u in range(BUF):
                        pool.wait_ge(ys_stored[u], 16 * (NBATCH // BUF))

        with ExitStack() as c:
            attend(c, 1)


_OUT = ((8, 1024, 128), "float32")


def kernel(**inputs):
    import numpy as _np
    import concourse.bacc as _bacc
    from concourse import mybir as _mybir
    from concourse.bass_utils import run_bass_kernel_spmd as _run

    a = {k.replace("L0_", ""): _np.asarray(v) for k, v in inputs.items()}
    heads = 8
    wg = a["ffn_w_gate"].transpose(0, 2, 1)
    wd = a["ffn_w_down"].transpose(0, 2, 1)
    half = wd.shape[2] // 2
    wd = _np.concatenate([wd[:, :, :half], wd[:, :, half:]], axis=1)
    laid = {
        "x": a["attn_x"],
        "w_dispT": a["attn_W_disp"].T,
        "w_val": a["attn_W_val"],
        "relT": a["attn_rel_pos_emb"].T,
        "w_strain": _np.tile(a["attn_W_strain"], (heads, 1)),
        "w_pos": _np.tile(a["attn_W_pos"], (1, heads)),
        "w_bond": _np.tile(a["attn_W_bond"], (heads, 1)),
        "w_dmg": _np.tile(a["attn_W_dmg"], (heads, 1)),
        "b_dmg": _np.tile(a["attn_b_dmg"][:, None], (heads, 1)),
        "w_dmg_out": _np.tile(a["attn_W_dmg_out"], (heads, 1)),
        "b_dmg_out": _np.tile(a["attn_b_dmg_out"][:, None], (128, 1)),
        "w_cproj": a["attn_W_cproj"],
        "router_wT": a["ffn_router_w"].T,
        "expert_bias": a["ffn_expert_bias"],
        "w_expert": _np.concatenate([wg, wd], axis=2),
        "w_gate_sharedT": a["ffn_w_gate_shared"].T,
        "w_down_sharedT": a["ffn_w_down_shared"].T,
    }
    nc = _bacc.Bacc("TRN2", target_bir_lowering=False, num_devices=1)
    arrays, args = {}, []
    for name, v in laid.items():
        arrays[f"in_{name}"] = _np.ascontiguousarray(v)
        args.append(nc.dram_tensor(f"in_{name}", v.shape, _mybir.dt.from_np(v.dtype), kind="ExternalInput").ap())
    args.append(nc.dram_tensor("out_0", _OUT[0], _mybir.dt.from_np(_np.dtype(_OUT[1])), kind="ExternalOutput").ap())
    moe_attention_layer(nc, *args)
    r = _run(nc, [arrays], core_ids=[0])
    return r.results[0]["out_0"]
```
